# Optimizing a Trainium2 kernel written in Bass

```python
import numpy as np
import jax
import jax.numpy as jnp

def _softmax(x, axis=-1):
    return jax.nn.softmax(x, axis=axis)

def _gelu(x):
    return jax.nn.gelu(x, approximate=True)

def _silu(x):
    return jax.nn.silu(x)

def _sigmoid(x):
    return jax.nn.sigmoid(x)

def _layernorm(x, axis=-1, eps=1e-05):
    m = jnp.mean(x, axis=axis, keepdims=True)
    v = jnp.var(x, axis=axis, keepdims=True)
    return (x - m) / jnp.sqrt(v + eps)

def _scatter_add(tgt, idx, src, axis=0):
    return tgt.at[idx].add(src)

def _segment_sum(src, seg, n):
    return jax.ops.segment_sum(src, seg, n)
kernel_name = 'mk_gnn_resnorm_d1_gnn_r8_f4eb6c'

def setup_inputs(seed: int=0):
    np.random.seed(seed)
    _w = jnp.asarray

    def _rec_inputs():
        import jax
        import jax.numpy as jnp
        _gk = jax.random.key(seed)
        x = -0.0005121 + 1.001 * jax.random.normal(jax.random.fold_in(_gk, 1), (12500, 64), jnp.float32)
        src = jax.random.randint(jax.random.fold_in(_gk, 2), (200000,), 0, 12500, jnp.int32)
        dst = jnp.minimum((12500 * jax.random.uniform(jax.random.fold_in(_gk, 3), (200000,)) ** 2.0).astype(jnp.int32), 99999)
        _o = jnp.argsort(dst, stable=True)
        src = src[_o]
        dst = dst[_o]
        edge_attr_32 = 0.000216709 + 1.00012 * jax.random.normal(jax.random.fold_in(_gk, 12), (200000, 32), jnp.float32)
        return (x, src, dst, edge_attr_32)
    x, src, dst, edge_attr_32 = _rec_inputs()

    def _L0_gnn_setup():
        import jax, jax.numpy as jnp
        import numpy as np
        N_NODES = 6250
        N_EDGES = 100000
        D_NODE = 64
        D_EDGE = 32
        D_HID = 128

        def _mlp(x, W1, b1, W2, b2):
            return jax.nn.relu(x @ W1 + b1) @ W2 + b2
        key = jax.random.key(seed)
        ks = jax.random.split(key, 12)
        inp = {'nodes': jax.random.normal(ks[0], (N_NODES, D_NODE), dtype=jnp.float32), 'row': jax.random.randint(ks[1], (N_EDGES,), 0, N_NODES, dtype=jnp.int32), 'col': jax.random.randint(ks[2], (N_EDGES,), 0, N_NODES, dtype=jnp.int32), 'edge_features': jax.random.normal(ks[3], (N_EDGES, D_EDGE), dtype=jnp.float32)}
        d_in_msg = 2 * D_NODE + D_EDGE
        inp['mW1'] = jax.random.normal(ks[4], (d_in_msg, D_HID), dtype=jnp.float32) / np.sqrt(d_in_msg)
        inp['mb1'] = jnp.zeros((D_HID,), dtype=jnp.float32)
        inp['mW2'] = jax.random.normal(ks[5], (D_HID, D_NODE), dtype=jnp.float32) / np.sqrt(D_HID)
        inp['mb2'] = jnp.zeros((D_NODE,), dtype=jnp.float32)
        d_in_upd = 2 * D_NODE
        inp['uW1'] = jax.random.normal(ks[6], (d_in_upd, D_HID), dtype=jnp.float32) / np.sqrt(d_in_upd)
        inp['ub1'] = jnp.zeros((D_HID,), dtype=jnp.float32)
        inp['uW2'] = jax.random.normal(ks[7], (D_HID, D_NODE), dtype=jnp.float32) / np.sqrt(D_HID)
        inp['ub2'] = jnp.zeros((D_NODE,), dtype=jnp.float32)
        return inp
    _L0_gnn_all = _L0_gnn_setup()
    _L0_gnn_in = {k: v for k, v in _L0_gnn_all.items() if k in ('mW1', 'mb1', 'mW2', 'mb2', 'uW1', 'ub1', 'uW2', 'ub2')}
    del _L0_gnn_all
    return {'x': x, 'src': src, 'dst': dst, 'edge_attr_32': edge_attr_32, 'L0_gnn_mW1': _L0_gnn_in['mW1'], 'L0_gnn_mb1': _L0_gnn_in['mb1'], 'L0_gnn_mW2': _L0_gnn_in['mW2'], 'L0_gnn_mb2': _L0_gnn_in['mb2'], 'L0_gnn_uW1': _L0_gnn_in['uW1'], 'L0_gnn_ub1': _L0_gnn_in['ub1'], 'L0_gnn_uW2': _L0_gnn_in['uW2'], 'L0_gnn_ub2': _L0_gnn_in['ub2']}

def reference(x, src, dst, edge_attr_32, L0_gnn_mW1, L0_gnn_mb1, L0_gnn_mW2, L0_gnn_mb2, L0_gnn_uW1, L0_gnn_ub1, L0_gnn_uW2, L0_gnn_ub2):
    import jax
    import jax.numpy as jnp

    def _L0_gnn_ref(nodes, row, col, edge_features, mW1, mb1, mW2, mb2, uW1, ub1, uW2, ub2):
        import jax, jax.numpy as jnp
        import numpy as np
        N_NODES = 6250
        N_EDGES = 100000
        D_NODE = 64
        D_EDGE = 32
        D_HID = 128

        def _mlp(x, W1, b1, W2, b2):
            return jax.nn.relu(x @ W1 + b1) @ W2 + b2
        msg_in = jnp.concatenate([nodes[row], nodes[col], edge_features], axis=-1)
        messages = _mlp(msg_in, mW1, mb1, mW2, mb2)
        aggregated = jax.ops.segment_sum(messages, col, num_segments=nodes.shape[0])
        upd_in = jnp.concatenate([nodes, aggregated], axis=-1)
        return _mlp(upd_in, uW1, ub1, uW2, ub2)
    x = _layernorm(x + _L0_gnn_ref(x, src, dst, edge_attr_32, L0_gnn_mW1, L0_gnn_mb1, L0_gnn_mW2, L0_gnn_mb2, L0_gnn_uW1, L0_gnn_ub1, L0_gnn_uW2, L0_gnn_ub2), axis=-1)
    return x

_drawn_inputs = setup_inputs


def setup_inputs(seed=0):
    import zlib

    import numpy as np

    out = dict(_drawn_inputs(seed))
    spreads = {'L0_gnn_mb1': (0.0, 0.1),
     'L0_gnn_mb2': (0.0, 0.1),
     'L0_gnn_ub1': (0.0, 0.311),
     'L0_gnn_ub2': (0.0, 0.1)}
    factors = {}
    for name, (base, spread) in spreads.items():
        noise = np.random.default_rng([zlib.crc32(name.encode()), seed]).standard_normal(out[name].shape)
        drawn = base * np.exp(spread * noise) if base else spread * noise
        out[name] = jnp.asarray(drawn.astype(out[name].dtype))
    for name, factor in factors.items():
        out[name] = (out[name] * factor).astype(out[name].dtype)
    return out
```

```python
import concourse.bass as bass
from concourse import mybir
from contextlib import ExitStack

N_NODES = 12500
N_EDGES = 200000
D = 64
DE = 32
DH = 128
P = 128

TPG = 4
GE = TPG * P
UNROLL = 8
GROUPS = -(-N_EDGES // (GE * UNROLL)) * UNROLL
ITERS = GROUPS // UNROLL
EDGES = GROUPS * GE
TILES = GROUPS * TPG
GPP = 4
GROWS = GROUPS // GPP
WIN = 96
BLOCKS = -(-N_NODES // P)
NODES = BLOCKS * P
LAST_BASE = NODES - WIN
RING = 4
KX = D + DE + 1
TRASH = NODES
AGG_ROWS = NODES + P
AGG_W = DH + 1
CB = 7
CHUNKS = BLOCKS // CB
HALF = CB * P // 2
TBL = 4
EPS = 1e-5
assert EDGES == TILES * P and GROWS * GPP == GROUPS and CHUNKS * CB == BLOCKS and CHUNKS % 2 == 0


def build(nc, x_rows, x_t, src_first, src_all, dst_groups, dst_tiles, edge_t,
          mw1, mb1, mw2, mb2, uw1, ub1, uw2, ub2, out):
    f32 = mybir.dt.float32
    i32 = mybir.dt.int32
    bf16 = mybir.dt.bfloat16
    ALU = mybir.AluOpType
    ACT = mybir.ActivationFunctionType
    X = mybir.AxisListType.X
    ds = bass.ds
    ET = mybir.EngineType

    ctx = ExitStack()
    with ctx:
        def sb(name, shape, dt=f32):
            return ctx.enter_context(nc.sbuf_tensor(name, shape, dt))

        def sem(name):
            return ctx.enter_context(nc.semaphore(name))

        def dram(name, shape, dt=f32):
            return nc.dram_tensor(name, shape, dt, kind="Internal").ap()

        table = dram("dst_table", (NODES, DH))
        base_i_dram = dram("window_base_i", (GROUPS,), i32)
        base_f_dram = dram("window_base_f", (GROUPS,))
        spread_dram = dram("window_spread", (GROUPS,))
        agg_dram = dram("agg_rows", (AGG_ROWS, AGG_W))

        ident = sb("ident", [P, P])
        iota_i = sb("iota_i", [P, WIN], i32)
        iota = sb("iota", [P, WIN])
        ones_bf = sb("ones_bf", [P, P], bf16)
        eps = sb("eps", [P, 1])
        w_xe = sb("w_xe", [KX, DH])
        w_dst = sb("w_dst", [D, DH])
        w2_pad = sb("w2_pad", [DH, P])
        b2_col = sb("b2_col", [P, 1])
        u1 = sb("u1", [2 * D, DH])
        c1_col = sb("c1_col", [DH, 1])
        u2 = sb("u2", [DH, D])
        c2_rows = sb("c2_rows", [P, D])

        agg_t = sb("agg_t", [DH, NODES])
        xc = sb("xc", [P, NODES])
        resid = sb("resid", [P, BLOCKS * D])

        src_idx = sb("src_idx", [P, TILES + TPG], i32)
        slot_idx = sb("slot_idx", [P, UNROLL * TPG], i32)
        dst_i = sb("dst_i", [P, TILES], i32)
        rel = sb("rel", [P, TILES])
        base_row = sb("base_row", [1, GROUPS], i32)
        spread_row = sb("spread_row", [1, GROUPS])
        spread_max = sb("spread_max", [1, 1], i32)
        base_mn = sb("base_mn", [GROWS, GPP])
        base_f = sb("base_f", [GROWS, GPP])
        base_i = sb("base_i", [GROWS, GPP], i32)
        dst_mx = sb("dst_mx", [GROWS, GPP])
        spread = sb("spread", [GROWS, GPP])

        xg = sb("xg", [P, UNROLL, TPG * D])
        xe = sb("xe", [KX, RING, GE])
        win_tab = sb("win_tab", [WIN, RING, DH])
        oh = sb("oh", [P, RING, TPG * WIN])
        oh_t = sb("oh_t", [WIN, 2, GE])
        hid = sb("hid", [P, 2, TPG * DH])

        dst_g = resid[0:GROWS, 0:GPP * GE].bitcast(i32)
        dst_g_real = resid[0:GROWS, GPP * GE:2 * GPP * GE]
        base_all = resid[:, 2 * GPP * GE:2 * GPP * GE + GROUPS]
        tab_out = [hid[:, 0, :], hid[:, 1, :]]

        banks = [ctx.enter_context(nc.psum_tensor(f"bank{i}", [P, 512], f32)) for i in range(8)]
        ps_x, ps_o, ps_h, ps_a = banks[0:2], banks[2:4], banks[4:6], banks[6:8]

        s_first = sem("s_first")
        s_src = sem("s_src")
        s_dstg = sem("s_dstg")
        s_dstt = sem("s_dstt")
        s_wmsg = sem("s_wmsg")
        s_wdst = sem("s_wdst")
        s_wupd = sem("s_wupd")
        s_xt = [sem("s_xt0"), sem("s_xt1")]
        s_resid = sem("s_resid")
        s_const = sem("s_const")
        s_iota = sem("s_iota")
        s_ident = sem("s_ident")
        s_iotaf = sem("s_iotaf")
        s_zero_dve = sem("s_zero_dve")
        s_zero_act = sem("s_zero_act")
        s_zero_w2 = sem("s_zero_w2")
        s_one_row = sem("s_one_row")
        s_win = sem("s_win")
        s_base = sem("s_base")
        s_scratch = sem("s_scratch")
        s_back = sem("s_back")
        s_flag = sem("s_flag")
        s_rel = sem("s_rel")
        s_tab_mm = sem("s_tab_mm")
        s_tab_cp = sem("s_tab_cp")
        s_tab_st = [sem("s_tab_st0"), sem("s_tab_st1")]
        s_gathered = [sem(f"s_gathered{i}") for i in range(UNROLL)]
        s_edge = [sem(f"s_edge{i}") for i in range(RING)]
        s_wtab = [sem(f"s_wtab{i}") for i in range(RING)]
        s_idx = sem("s_idx")
        s_opened = sem("s_opened")
        s_xt_mm = sem("s_xt_mm")
        s_xe = sem("s_xe")
        s_oh = sem("s_oh")
        s_oht_mm = sem("s_oht_mm")
        s_oht = sem("s_oht")
        s_h = sem("s_h")
        s_relu = sem("s_relu")
        s_agg = sem("s_agg")
        s_added = sem("s_added")
        s_edges_done = sem("s_edges_done")
        s_c2 = sem("s_c2")
        s_m1 = sem("s_m1")
        s_u = sem("s_u")
        s_m2 = sem("s_m2")
        s_hu = sem("s_hu")
        s_m3 = sem("s_m3")
        s_sum = sem("s_sum")
        s_mean = sem("s_mean")
        s_red = sem("s_red")
        s_dev = sem("s_dev")
        s_sq = sem("s_sq")
        s_var = sem("s_var")
        s_std = sem("s_std")
        s_rstd = sem("s_rstd")
        s_norm = sem("s_norm")
        s_out = [sem("s_out0"), sem("s_out1")]

        def wait(eng, s, n):
            if not isinstance(n, int) or n > 0:
                eng.wait_ge(s, n)

        def gather(pool, g, k):
            wait(pool, s_idx, g - UNROLL + 1)
            pool.sem_inc(s_opened, 1)
            for j in range(TPG):
                c = k * TPG + j
                pool.indirect_dma_start(
                    out=xg[:, k, j * D:(j + 1) * D], out_offset=None, in_=x_rows,
                    in_offset=bass.IndirectOffsetOnAxis(ap=slot_idx[:, c:c + 1], axis=0),
                ).then_inc(s_gathered[k], 16)

        def load_operands(sp, g, k, base):
            r = k % RING
            wait(sp, s_h, g - RING + 1)
            sp.dma_start(xe[D:D + DE, r, :], edge_t[:, ds(g * GE, GE)]).then_inc(s_edge[r], 16)
            sp.dma_start(win_tab[:, r, :], table[ds(base, WIN), :]).then_inc(s_wtab[r], 16)

        def transpose_x(pe, g, k, lap):
            q = k % 2
            wait(pe, s_gathered[k], (lap + 1) * 16 * TPG)
            wait(pe, s_xe, g - 1)
            for m in range(TPG // 2):
                last = nc.tensor.transpose(ps_x[q][:, m * P:(m + 1) * P],
                                           xg[:, k, m * 2 * D:(m + 1) * 2 * D], ident[:, :])
            last.then_inc(s_xt_mm, 1)

        def transpose_oh(pe, g, k):
            q, r = k % 2, k % RING
            wait(pe, s_oh, g + 1)
            wait(pe, s_oht, g - 1)
            for j in range(TPG):
                last = nc.tensor.transpose(ps_o[q][0:WIN, j * P:(j + 1) * P],
                                           oh[:, r, j * WIN:(j + 1) * WIN], ident[:, :])
            last.then_inc(s_oht_mm, 1)

        def hidden(pe, g, k, lap):
            q, r = k % 2, k % RING
            n = lap * (UNROLL // RING) + k // RING + 1
            wait(pe, s_xe, g + 1)
            wait(pe, s_edge[r], n * 16)
            wait(pe, s_wtab[r], n * 16)
            wait(pe, s_oht, g + 1)
            wait(pe, s_relu, g - 1)
            for j in range(TPG):
                o = ps_h[q][:, j * DH:(j + 1) * DH]
                nc.tensor.matmul(o, xe[:, r, j * P:(j + 1) * P], w_xe[:, :], start=True, stop=False)
                last = nc.tensor.matmul(o, oh_t[:, q, j * P:(j + 1) * P], win_tab[:, r, :],
                                        start=False, stop=True)
            last.then_inc(s_h, 1)

        def aggregate(pe, g, k):
            q, r = k % 2, k % RING
            wait(pe, s_relu, g + 1)
            wait(pe, s_added, g - 1)
            for j in range(TPG):
                nc.tensor.matmul(ps_a[q][:, 0:WIN], hid[:, q, j * DH:(j + 1) * DH],
                                 oh[:, r, j * WIN:(j + 1) * WIN], start=(j == 0), stop=(j == TPG - 1))
            half = oh[:, r, :].bitcast(bf16).rearrange("p (n two) -> p n two", two=2)
            for j in range(TPG):
                last = nc.tensor.matmul(ps_a[q][:, WIN:2 * WIN], ones_bf[:, :],
                                        half[:, j * WIN:(j + 1) * WIN, 1],
                                        start=(j == 0), stop=(j == TPG - 1))
            last.then_inc(s_agg, 1)

        def copy_x(g, k):
            act = nc.scalar
            q, r = k % 2, k % RING
            wait(act, s_xt_mm, g + 1)
            wait(act, s_h, g - RING + 1)
            to = xe[0:D, r, :].rearrange("p (m t e) -> p m t e", t=2, e=P)
            for t in range(2):
                of = ps_x[q][t * D:(t + 1) * D, 0:GE // 2].rearrange("p (m e) -> p m e", e=P)
                last = act.activation(to[:, :, t, :], of, ACT.Copy)
            last.then_inc(s_xe, 1)

        def relu(g, k):
            act = nc.scalar
            q = k % 2
            wait(act, s_h, g + 1)
            wait(act, s_agg, g - 1)
            act.activation(hid[:, q, :], ps_h[q][:, :], ACT.Relu).then_inc(s_relu, 1)

        def one_hot(g, k):
            dve = nc.vector
            r = k % RING
            wait(dve, s_agg, g - RING + 1)
            grid = [P, TPG, WIN]
            dve.tensor_tensor(oh[:, r, :].rearrange("p (j w) -> p j w", w=WIN),
                              iota[:, None, :].to_broadcast(grid),
                              rel[:, ds(g * TPG, TPG)][:, :, None].to_broadcast(grid),
                              ALU.is_equal).then_inc(s_oh, 1)

        def copy_oh(g, k):
            dve = nc.vector
            q = k % 2
            wait(dve, s_oht_mm, g + 1)
            wait(dve, s_h, g - 1)
            dve.tensor_copy(oh_t[:, q, :], ps_o[q][0:WIN, :]).then_inc(s_oht, 1)

        def next_indices(g, k):
            dve = nc.vector
            wait(dve, s_xt_mm, g + 1)
            dve.tensor_copy(slot_idx[:, k * TPG:(k + 1) * TPG],
                            src_idx[:, ds((g + UNROLL) * TPG, TPG)]).then_inc(s_idx, 1)

        def add_window(g, k, base):
            dve = nc.vector
            q = k % 2
            wait(dve, s_agg, g + 1)
            wait(dve, s_added, g)
            to, cnt = agg_t[:, ds(base, WIN)], xc[D:P, ds(base, WIN)]
            dve.tensor_tensor(to, ps_a[q][:, 0:WIN], to, ALU.add)
            dve.tensor_tensor(cnt, ps_a[q][D:P, WIN:2 * WIN], cnt, ALU.add).then_inc(s_added, 1)

        def window_bases(eng, start, n):
            return nc.values_load_multi_w_load_instructions(
                base_row[0:1, ds(start, n)], engines=(eng,), min_val=0, max_val=LAST_BASE,
                skip_runtime_bounds_check_because="the chip clamps them to this range")[1]

        def table_stored(eng):
            for n in range(2):
                eng.wait_ge(s_tab_st[n], (BLOCKS // 2 + 1 - n) // 2 * 16)

        def laps(eng, lap):
            lap(0)
            with eng.Fori(1, ITERS - 1) as i:
                lap(i)
            lap(ITERS - 1)

        def fast(eng, body, other):
            eng.wait_ge(s_flag, 1)
            widest = eng.value_load(spread_max[0:1, 0:1], min_val=0, max_val=NODES)
            with eng.If(widest < WIN):
                body()
            with eng.Else():
                other()

        g_x = xg[:, 0, 0:P]
        g_tab = hid[:, 0, 0:DH]
        g_dcol = rel[:, 0:1]
        g_dbc = hid[:, 0, DH:2 * DH]
        g_same = hid[:, 0, 2 * DH:3 * DH]
        g_low = hid[:, 0, 3 * DH:4 * DH]
        g_pre = hid[:, 1, 0:DH]
        g_h = oh[:, 0, 0:AGG_W]
        g_sum = oh[:, 1, 0:AGG_W]
        g_earlier = hid[:, 1, 2 * DH:3 * DH]
        g_scr = rel[:, 8:16]
        g_xe = xe[:, 0, 0:P]
        g_back = oh[:, 2, 0:AGG_W]
        g_cbc = hid[:, 1, 3 * DH:4 * DH]
        g_si, g_di, g_to = slot_idx[:, 0:1], slot_idx[:, 1:2], slot_idx[:, 2:3]
        t_zero = sem("t_zero")
        t_init = sem("t_init")
        t_low = sem("t_low")
        t_gat = sem("t_gat")
        t_edge = sem("t_edge")
        t_tr = sem("t_tr")
        t_xe = sem("t_xe")
        t_h = sem("t_h")
        t_same = sem("t_same")
        t_pre = sem("t_pre")
        t_relu = sem("t_relu")
        t_sum = sem("t_sum")
        t_step = sem("t_step")
        t_out = sem("t_out")
        t_scat = sem("t_scat")
        t_rows = sem("t_rows")
        t_cbc = sem("t_cbc")
        t_btr = sem("t_btr")
        t_bcp = sem("t_bcp")
        DVE_STEPS = 4

        def general_pool():
            pool = nc.gpsimd
            for k in range(UNROLL):
                pool.wait_ge(s_gathered[k], 16 * TPG)
            table_stored(pool)
            pool.memset(g_x[:, D:P], 0.0).then_inc(t_zero, 1)
            pool.memset(g_low, 1.0).then_inc(t_low, 1)
            pool.wait_ge(t_low, 1)
            pool.affine_select(out=g_low, in_=g_low, compare_op=ALU.is_gt, fill=0.0, base=0,
                               pattern=[[-1, P]], channel_multiplier=1).then_inc(t_low, 1)
            with pool.Fori(0, TILES) as t:
                pool.wait_ge(t_step, t * DVE_STEPS + 1)
                pool.sem_inc(s_opened, 1)
                pool.indirect_dma_start(
                    out=g_x[:, 0:D], out_offset=None, in_=x_rows,
                    in_offset=bass.IndirectOffsetOnAxis(ap=g_si, axis=0)).then_inc(t_gat, 16)
                pool.indirect_dma_start(
                    out=g_tab, out_offset=None, in_=table,
                    in_offset=bass.IndirectOffsetOnAxis(ap=g_di, axis=0)).then_inc(t_gat, 16)
                pool.wait_ge(t_out, t + 1)
                pool.sem_inc(s_opened, 1)
                pool.indirect_dma_start(
                    out=agg_dram, out_offset=bass.IndirectOffsetOnAxis(ap=g_to, axis=0),
                    in_=g_sum, in_offset=None, compute_op=ALU.add).then_inc(t_scat, 16)

        def general_sync():
            sp = nc.sync
            half = AGG_ROWS * AGG_W // P // 2
            rows = agg_dram.rearrange("(p r) w -> p (r w)", p=P)
            sp.wait_ge(s_zero_act, 1)
            at = 0
            for n in (half, rows.shape[1] - half):
                sp.dma_start(rows[:, at:at + n], agg_t[:, 0:n]).then_inc(t_init, 16)
                at += n
            with sp.Fori(0, TILES) as t:
                sp.wait_ge(t_step, t * DVE_STEPS + 1)
                sp.dma_start(g_xe[D:D + DE, :], edge_t[:, ds(t * P, P)]).then_inc(t_edge, 16)
            sp.wait_ge(t_scat, TILES * 16)
            with sp.Fori(0, BLOCKS) as b:
                sp.wait_ge(t_bcp, b + 1)
                sp.dma_start(g_back, agg_dram[ds(b * P, P), :]).then_inc(t_rows, 16)

        def general_tensor():
            pe = nc.tensor
            pe.wait_ge(t_zero, 1)
            with pe.Fori(0, TILES) as t:
                pe.wait_ge(t_gat, (t + 1) * 32)
                pe.wait_ge(t_step, t * DVE_STEPS + 2)
                nc.tensor.transpose(ps_x[0][:, 0:P], g_x, ident[:, :])
                nc.tensor.transpose(ps_o[0][:, 0:P], g_dbc, ident[:, :]).then_inc(t_tr, 1)
                pe.wait_ge(t_xe, t + 1)
                pe.wait_ge(t_edge, (t + 1) * 16)
                nc.tensor.matmul(ps_h[0][:, 0:DH], g_xe, w_xe[:, :],
                                 start=True, stop=True).then_inc(t_h, 1)
                pe.wait_ge(t_same, t + 1)
                pe.wait_ge(t_relu, t + 1)
                nc.tensor.matmul(ps_a[0][:, 0:AGG_W], g_same, g_h,
                                 start=True, stop=True).then_inc(t_sum, 1)
            with pe.Fori(0, BLOCKS) as b:
                pe.wait_ge(t_cbc, b + 1)
                nc.tensor.transpose(ps_x[0][:, 0:P], g_back[:, 0:DH], ident[:, :])
                nc.tensor.transpose(ps_o[0][:, 0:P], g_cbc, ident[:, :]).then_inc(t_btr, 1)

        def general_scalar():
            act = nc.scalar
            with act.Fori(0, TILES) as t:
                act.wait_ge(t_tr, t + 1)
                act.activation(g_xe[0:D, :], ps_x[0][0:D, 0:P], ACT.Copy).then_inc(t_xe, 1)
                act.wait_ge(t_pre, t + 1)
                act.activation(g_h[:, 0:DH], g_pre, ACT.Relu).then_inc(t_relu, 1)

        def general_vector():
            dve = nc.vector
            table_stored(dve)
            dve.wait_ge(s_src, 16)
            dve.wait_ge(t_low, 2)
            dve.wait_ge(t_init, 32)
            dve.memset(g_h[:, DH:AGG_W], 1.0).then_inc(t_bcp, 1)
            dve.wait_ge(t_bcp, 1)
            with dve.Fori(0, TILES) as t:
                at = t * DVE_STEPS
                dve.tensor_copy(g_si, src_idx[:, ds(t, 1)])
                dve.tensor_copy(g_dcol, dst_i[:, ds(t, 1)])
                dve.tensor_copy(g_di, dst_i[:, ds(t, 1)]).then_inc(t_step, 1)
                dve.wait_ge(t_step, at + 1)
                dve.tensor_copy(g_dbc, g_dcol.to_broadcast([P, P])).then_inc(t_step, 1)
                dve.wait_ge(t_tr, t + 1)
                dve.tensor_scalar(g_same, ps_o[0][:, 0:P], g_dcol, None, ALU.is_equal).then_inc(t_same, 1)
                dve.wait_ge(t_h, t + 1)
                dve.tensor_tensor(g_pre, ps_h[0][:, 0:DH], g_tab, ALU.add).then_inc(t_pre, 1)
                dve.wait_ge(t_same, t + 1)
                dve.tensor_tensor(g_earlier, g_same, g_low, ALU.mult).then_inc(t_step, 1)
                dve.wait_ge(t_step, at + 3)
                dve.reduce_max(g_scr[:, 0:1], g_earlier, X).then_inc(t_step, 1)
                dve.wait_ge(t_step, at + 4)
                general_row(dve, t)
                dve.wait_ge(t_sum, t + 1)
                dve.tensor_copy(g_sum, ps_a[0][:, 0:AGG_W]).then_inc(t_out, 1)
                dve.wait_ge(t_scat, (t + 1) * 16)

            with dve.Fori(0, BLOCKS) as b:
                dve.wait_ge(t_rows, (b + 1) * 16)
                dve.tensor_copy(g_cbc, g_back[:, DH:AGG_W].to_broadcast([P, P])).then_inc(t_cbc, 1)
                dve.wait_ge(t_btr, b + 1)
                dve.tensor_copy(agg_t[:, ds(b * P, P)], ps_x[0][:, 0:P])
                dve.tensor_copy(xc[D:P, ds(b * P, P)], ps_o[0][D:P, 0:P]).then_inc(t_bcp, 1)
            dve.wait_ge(t_bcp, BLOCKS + 1)

        t_row = sem("t_row")
        trash_f = sb("trash_f", [P, 1])
        trash_i = sb("trash_i", [P, 1], i32)

        def general_row(dve, t):
            dve.tensor_tensor(g_scr[:, 1:2], trash_f[:, :], g_dcol, ALU.subtract).then_inc(t_row, 1)
            dve.wait_ge(t_row, t * 2 + 1)
            dve.tensor_tensor(g_scr[:, 2:3], g_scr[:, 1:2], g_scr[:, 0:1], ALU.mult).then_inc(t_row, 1)
            dve.wait_ge(t_row, t * 2 + 2)
            dve.tensor_tensor(g_to, g_scr[:, 2:3], g_dcol, ALU.add)

        xg_flat = xg[:, :, :].rearrange("p a b -> p (a b)")
        hu = [xg_flat[:, 0:2 * HALF], xg_flat[:, 2 * HALF:4 * HALF]]
        CW = CB * D
        sq = [oh[:, :, :].rearrange("p a b -> p (a b)")[:, n * CW:(n + 1) * CW] for n in range(2)]
        outb = [hid[:, n, 0:CW] for n in range(2)]
        stat = sb("stat", [P, 4, 4 * CB])

        def st(c4, n):
            return stat[:, c4, n * CB:(n + 1) * CB]

        def units(c, h):
            return ds(c * (2 * HALF) + h * HALF, HALF)

        def m1(pe, c, p):
            for h in range(2):
                wait(pe, s_u, (c - 1) * 2 + h + 1)
                nc.tensor.matmul(banks[h][:, 0:HALF], w2_pad[:, :], agg_t[:, units(c, h)],
                                 start=True, stop=True).then_inc(s_m1, 1)

        def m2(pe, c, p):
            for h in range(2):
                wait(pe, s_u, c * 2 + h + 1)
                wait(pe, s_hu, (c - 1) * 2 + h + 1)
                nc.tensor.matmul(banks[2 + h][:, 0:HALF], u1[:, :], xc[:, units(c, h)],
                                 start=True, stop=True).then_inc(s_m2, 1)

        def m3(pe, c, p):
            wait(pe, s_hu, c * 2 + 2)
            wait(pe, s_sum, c - 1)
            for b in range(CB):
                last = nc.tensor.matmul(banks[4 + p][:, b * D:(b + 1) * D],
                                        hu[p][:, b * P:(b + 1) * P], u2[:, :], start=True, stop=True)
            last.then_inc(s_m3, 1)

        def stack_agg(c, p):
            dve = nc.vector
            for h in range(2):
                wait(dve, s_m1, c * 2 + h + 1)
                cnt = xc[D:P, units(c, h)]
                dve.scalar_tensor_tensor(cnt, cnt, b2_col[D:P, 0:1], banks[h][D:P, 0:HALF],
                                         ALU.mult, ALU.add).then_inc(s_u, 1)

        def relu_upd(c, p):
            act = nc.scalar
            for h in range(2):
                wait(act, s_m2, c * 2 + h + 1)
                wait(act, s_m3, c - 1)
                act.activation(hu[p][:, h * HALF:(h + 1) * HALF], banks[2 + h][:, 0:HALF], ACT.Relu,
                               bias=c1_col[:, 0:1]).then_inc(s_hu, 1)

        def chunk(t, c, w=CW):
            return t[:, ds(c * w, w)]

        def blocks(ap):
            return ap.rearrange("p (b d) -> p b d", d=D)

        def center(c, p, r):
            dve = nc.vector
            y = chunk(resid, c)
            wait(dve, s_norm, c - 3)
            wait(dve, s_m3, c + 1)
            dve.tensor_tensor(y, banks[4 + p][:, 0:CW], y, ALU.add).then_inc(s_sum, 1)
            wait(dve, s_sum, c + 1)
            dve.reduce_sum(st(r, 0), blocks(y), X).then_inc(s_red, 1)
            wait(dve, s_red, c + 1)
            dve.tensor_scalar(st(r, 1), st(r, 0), 1.0 / D, None, ALU.mult).then_inc(s_mean, 1)
            wait(dve, s_mean, c + 1)
            dve.tensor_tensor(blocks(y), blocks(y), st(r, 1)[:, :, None].to_broadcast([P, CB, D]),
                              ALU.subtract).then_inc(s_dev, 1)

        def square(c, p):
            act = nc.scalar
            wait(act, s_dev, c + 1)
            wait(act, s_var, c - 1)
            act.activation(sq[p], chunk(resid, c), ACT.Square).then_inc(s_sq, 1)

        def variance(c, p, r):
            dve = nc.vector
            wait(dve, s_sq, c + 1)
            dve.reduce_sum(st(r, 2), blocks(sq[p]), X).then_inc(s_var, 1)

        def deviation(c, r):
            act = nc.scalar
            wait(act, s_var, c + 1)
            act.activation(st(r, 3), st(r, 2), ACT.Sqrt, bias=eps[:, 0:1], scale=1.0 / D).then_inc(s_std, 1)

        def inverse(c, r):
            dve = nc.vector
            wait(dve, s_std, c + 1)
            dve.reciprocal(st(r, 0), st(r, 3)).then_inc(s_rstd, 1)

        def normalize(pool, c, p, r):
            wait(pool, s_rstd, c + 1)
            pool.tensor_tensor(blocks(outb[p]), blocks(chunk(resid, c)),
                               st(r, 0)[:, :, None].to_broadcast([P, CB, D]), ALU.mult).then_inc(s_norm, 1)

        block = ctx.enter_context(nc.Block())

        @block.gpsimd
        def _(pool):
            pool.iota(iota_i[:, :], pattern=[[1, WIN]], base=0, channel_multiplier=0).then_inc(s_iota, 1)
            pool.memset(ident[:, :], 0.0).then_inc(s_ident, 1)
            pool.wait_ge(s_ident, 1)
            pool.affine_select(out=ident[:, :], in_=ident[:, :], compare_op=ALU.not_equal, fill=1.0,
                               base=0, pattern=[[-1, P]], channel_multiplier=1).then_inc(s_ident, 1)
            pool.iota(trash_i[:, :], pattern=[[0, 1]], base=TRASH, channel_multiplier=1).then_inc(s_iota, 1)
            pool.wait_ge(s_first, 16)
            for k in range(UNROLL):
                gather(pool, k, k)

            def windowed():
                def lap(i):
                    for k in range(UNROLL):
                        gather(pool, i * UNROLL + k, k)
                with pool.Fori(1, ITERS) as i:
                    lap(i)

            fast(pool, windowed, general_pool)

            def norm(c, p, r):
                if not isinstance(c, int) or c >= 2:
                    pool.wait_ge(s_out[p], (c - p) * 8)
                normalize(pool, c, p, r)
            for c in range(CHUNKS):
                norm(c, c % 2, c % 4)

        @block.sync
        def _(sp):
            sp.dma_start(slot_idx[:, :], src_first).then_inc(s_first, 16)
            sp.dma_start(dst_g, dst_groups).then_inc(s_dstg, 16)
            sp.dma_start(dst_i[:, :], dst_tiles).then_inc(s_dstt, 16)
            sp.dma_start(src_idx[:, 0:TILES], src_all).then_inc(s_src, 16)
            sp.wait_ge(s_win, 4)
            sp.dma_start(base_i_dram.rearrange("(p g) -> p g", g=GPP), base_i[:, :]).then_inc(s_scratch, 16)
            sp.dma_start(base_f_dram.rearrange("(p g) -> p g", g=GPP), base_f[:, :]).then_inc(s_scratch, 16)
            sp.dma_start(spread_dram.rearrange("(p g) -> p g", g=GPP), spread[:, :]).then_inc(s_scratch, 16)
            sp.wait_ge(s_scratch, 48)
            sp.dma_start(base_all, base_f_dram[None, :].to_broadcast([P, GROUPS])).then_inc(s_back, 16)
            sp.dma_start(spread_row[:, :], spread_dram[None, :]).then_inc(s_back, 16)
            sp.dma_start(base_row[:, :], base_i_dram[None, :]).then_inc(s_back, 16)
            tab = table.rearrange("(s b p) n -> s p b n", p=P, b=2)
            for n in range(BLOCKS // 2):
                sp.wait_ge(s_tab_cp, n + 1)
                sp.dma_start(tab[n], tab_out[n % 2][:, 0:2 * DH].rearrange("p (b n) -> p b n", n=DH)
                             ).then_inc(s_tab_st[n % 2], 16)
            table_stored(sp)
            sp.wait_ge(s_back, 48)

            def load_resid():
                main = BLOCKS - 1
                sp.wait_ge(s_rel, 1)
                sp.dma_start(resid[:, 0:main * D].rearrange("p (b d) -> p b d", d=D),
                             x_rows[0:main * P, :].rearrange("(b p) d -> p b d", p=P)
                             ).then_inc(s_resid, 16)
                sp.dma_start(resid[0:N_NODES - main * P, main * D:], x_rows[main * P:, :]
                             ).then_inc(s_resid, 16)

            def windowed():
                def lap(i):
                    bases = window_bases(ET.SP, i * UNROLL, UNROLL)
                    for k in range(UNROLL):
                        load_operands(sp, i * UNROLL + k, k, bases[k])
                lap(0)
                load_resid()
                with sp.Fori(1, ITERS) as i:
                    lap(i)

            def general():
                load_resid()
                general_sync()

            fast(sp, windowed, general)

            main = CHUNKS - 1
            for c in range(CHUNKS):
                sp.wait_ge(s_norm, c + 1)
                rows = c * CB * P
                nb = CB if c < main else CB - 1
                sp.dma_start(out[rows:rows + nb * P, :].rearrange("(b p) d -> p b d", p=P),
                             blocks(outb[c % 2])[:, 0:nb, :]).then_inc(s_out[c % 2], 16)
                if c == main:
                    tail = N_NODES - (BLOCKS - 1) * P
                    sp.dma_start(out[(BLOCKS - 1) * P:, :], outb[c % 2][0:tail, nb * D:]
                                 ).then_inc(s_out[c % 2], 16)
            sp.wait_ge(s_out[0], CHUNKS // 2 * 16)
            sp.wait_ge(s_out[1], (CHUNKS // 2 + 1) * 16)

        @block.scalar
        def _(act):
            for n, q in ((0, NODES // 4), (NODES // 4, NODES)):
                act.dma_start(xc[0:D, n:q], x_t[:, n:q]).then_inc(s_xt[int(n > 0)], 16)
            act.dma_start(w_dst[:, :], mw1[D:2 * D, :]).then_inc(s_wdst, 16)
            act.dma_start(w_xe[0:D, :], mw1[0:D, :]).then_inc(s_wmsg, 16)
            act.dma_start(w_xe[D:D + DE, :], mw1[2 * D:2 * D + DE, :]).then_inc(s_wmsg, 16)
            act.dma_start(w_xe[D + DE:KX, :], mb1[None, :]).then_inc(s_wmsg, 16)
            act.wait_ge(s_zero_w2, 1)
            act.dma_start(w2_pad[:, D:P], mw2).then_inc(s_wupd, 16)
            act.dma_start(b2_col[D:P, :], mb2[:, None]).then_inc(s_wupd, 16)
            act.dma_start(u1[:, :], uw1).then_inc(s_wupd, 16)
            act.dma_start(c1_col[:, :], ub1[:, None]).then_inc(s_wupd, 16)
            act.dma_start(u2[:, :], uw2).then_inc(s_wupd, 16)
            act.dma_start(c2_rows[:, :], ub2[None, :].to_broadcast([P, D])).then_inc(s_wupd, 16)
            act.memzero(agg_t[:, :]).then_inc(s_zero_act, 1)
            for n in range(BLOCKS // 2):
                act.wait_ge(s_tab_mm, n + 1)
                if n >= 2:
                    act.wait_ge(s_tab_st[n % 2], n // 2 * 16)
                act.activation(tab_out[n % 2][:, 0:2 * DH], banks[n % 2][:, 0:2 * DH],
                               ACT.Copy).then_inc(s_tab_cp, 1)

            def windowed():
                table_stored(act)
                copy_x(0, 0)

                def lap(i):
                    for k in range(UNROLL):
                        g = i * UNROLL + k
                        if not (isinstance(g, int) and g == GROUPS - 1):
                            copy_x(g + 1, (k + 1) % UNROLL)
                        relu(g, k)
                laps(act, lap)

            fast(act, windowed, general_scalar)
            for c in range(CHUNKS + 2):
                if c < CHUNKS:
                    relu_upd(c, c % 2)
                if 1 <= c <= CHUNKS:
                    square(c - 1, (c - 1) % 2)
                if c >= 2:
                    deviation(c - 2, (c - 2) % 4)

        @block.vector
        def _(dve):
            dve.memset(w2_pad[:, 0:D], 0.0).then_inc(s_zero_w2, 1)
            dve.memset(ones_bf[:, :], 1.0)
            dve.memset(src_idx[:, TILES:], 0)
            dve.memset(eps[:, :], EPS).then_inc(s_const, 1)
            dve.memset(xe[D + DE:KX, :, :], 1.0).then_inc(s_one_row, 1)
            dve.wait_ge(s_iota, 1)
            dve.tensor_copy(iota[:, :], iota_i[:, :]).then_inc(s_iotaf, 1)
            dve.wait_ge(s_iota, 2)
            dve.tensor_copy(trash_f[:, :], trash_i[:, :])
            dve.wait_ge(s_dstg, 16)
            dve.tensor_reduce(base_mn[:, :], dst_g.rearrange("p (g e) -> p g e", e=GE), X, ALU.min
                              ).then_inc(s_base, 1)
            dve.scalar_tensor_tensor(dst_g_real, dst_g, float(N_NODES), dst_g, ALU.is_lt, ALU.mult
                                     ).then_inc(s_base, 1)
            dve.wait_ge(s_base, 1)
            dve.tensor_scalar(base_f[:, :], base_mn[:, :], float(LAST_BASE), None, ALU.min
                              ).then_inc(s_win, 1)
            dve.wait_ge(s_base, 2)
            dve.reduce_max(dst_mx[:, :], dst_g_real.rearrange("p (g e) -> p g e", e=GE), X).then_inc(s_win, 1)
            dve.wait_ge(s_win, 2)
            dve.tensor_copy(base_i[:, :], base_f[:, :]).then_inc(s_win, 1)
            dve.tensor_tensor(spread[:, :], dst_mx[:, :], base_f[:, :], ALU.subtract).then_inc(s_win, 1)
            dve.memset(xc[D:P, :], 0.0)
            dve.memset(resid[:, (BLOCKS - 1) * D:], 0.0).then_inc(s_zero_dve, 1)
            dve.wait_ge(s_dstt, 16)
            dve.wait_ge(s_back, 48)
            grid = [P, GROUPS, TPG]
            dve.tensor_tensor(rel[:, :].rearrange("p (g j) -> p g j", j=TPG),
                              dst_i[:, :].rearrange("p (g j) -> p g j", j=TPG),
                              base_all[:, :, None].to_broadcast(grid), ALU.subtract).then_inc(s_rel, 1)
            dve.reduce_max(spread_max[:, :], spread_row[:, :], X).then_inc(s_flag, 1)

            def windowed():
                dve.wait_ge(s_rel, 1)
                dve.wait_ge(s_iotaf, 1)
                dve.wait_ge(s_src, 16)
                one_hot(0, 0)
                one_hot(1, 1)
                copy_oh(0, 0)
                next_indices(0, 0)
                dve.wait_ge(s_zero_act, 1)
                dve.wait_ge(s_zero_dve, 1)

                def lap(i):
                    if isinstance(i, int) and i == 0:
                        bases = [None, None, *window_bases(ET.DVE, 0, UNROLL - 2)]
                    else:
                        bases = window_bases(ET.DVE, i * UNROLL - 2, UNROLL)
                    for k in range(UNROLL):
                        g = i * UNROLL + k
                        known = isinstance(g, int)
                        if not (known and g + 2 >= GROUPS):
                            one_hot(g + 2, (k + 2) % UNROLL)
                        if not (known and g + 1 >= GROUPS):
                            copy_oh(g + 1, (k + 1) % UNROLL)
                        if not (known and g + 1 + UNROLL >= GROUPS):
                            next_indices(g + 1, (k + 1) % UNROLL)
                        if not (known and g < 2):
                            add_window(g - 2, (k - 2) % UNROLL, bases[k])
                laps(dve, lap)
                last = window_bases(ET.DVE, GROUPS - 2, 2)
                for n in range(2):
                    add_window(GROUPS - 2 + n, (UNROLL - 2 + n) % UNROLL, last[n])
                dve.wait_ge(s_added, GROUPS)

            def general():
                general_vector()

            fast(dve, windowed, general)
            dve.wait_ge(s_resid, 32)
            dve.wait_ge(s_wupd, 96)
            dve.tensor_tensor(blocks(resid[:, :]), blocks(resid[:, :]),
                              c2_rows[:, None, :].to_broadcast([P, BLOCKS, D]), ALU.add
                              ).then_inc(s_edges_done, 1)
            dve.wait_ge(s_edges_done, 1)
            stack_agg(0, 0)
            for c in range(CHUNKS + 3):
                if c + 1 < CHUNKS:
                    stack_agg(c + 1, (c + 1) % 2)
                if 1 <= c <= CHUNKS:
                    center(c - 1, (c - 1) % 2, (c - 1) % 4)
                if 2 <= c <= CHUNKS + 1:
                    variance(c - 2, (c - 2) % 2, (c - 2) % 4)
                if c >= 3:
                    inverse(c - 3, (c - 3) % 4)

        @block.tensor
        def _(pe):
            pe.wait_ge(s_wdst, 16)
            for n in range(BLOCKS // 2):
                if n == 0:
                    pe.wait_ge(s_xt[0], 16)
                if (n + 1) * 2 * P > NODES // 4 and n * 2 * P <= NODES // 4:
                    pe.wait_ge(s_xt[1], 16)
                wait(pe, s_tab_cp, n - 1)
                for b in range(2):
                    at = (n * 2 + b) * P
                    last = nc.tensor.matmul(banks[n % 2][:, b * DH:(b + 1) * DH], xc[0:D, at:at + P],
                                            w_dst[:, :], start=True, stop=True)
                last.then_inc(s_tab_mm, 1)

            def windowed():
                pe.wait_ge(s_ident, 2)
                pe.wait_ge(s_tab_cp, BLOCKS // 2)
                pe.wait_ge(s_wmsg, 48)
                pe.wait_ge(s_one_row, 1)
                pe.wait_ge(s_const, 1)
                transpose_x(pe, 0, 0, 0)
                transpose_oh(pe, 0, 0)

                def lap(i):
                    for k in range(UNROLL):
                        g = i * UNROLL + k
                        known = isinstance(g, int)
                        if not (known and g + 1 >= GROUPS):
                            transpose_x(pe, g + 1, (k + 1) % UNROLL, i + (k + 1) // UNROLL)
                            transpose_oh(pe, g + 1, (k + 1) % UNROLL)
                        hidden(pe, g, k, i)
                        if not (known and g == 0):
                            aggregate(pe, g - 1, (k - 1) % UNROLL)
                laps(pe, lap)
                aggregate(pe, GROUPS - 1, UNROLL - 1)

            def general():
                pe.wait_ge(s_ident, 2)
                pe.wait_ge(s_tab_cp, BLOCKS // 2)
                pe.wait_ge(s_wmsg, 48)
                pe.wait_ge(s_one_row, 1)
                general_tensor()

            fast(pe, windowed, general)
            pe.wait_ge(s_wupd, 96)
            pe.wait_ge(s_edges_done, 1)
            m1(pe, 0, 0)
            for c in range(CHUNKS + 1):
                if c + 1 < CHUNKS:
                    m1(pe, c + 1, (c + 1) % 2)
                if c < CHUNKS:
                    m2(pe, c, c % 2)
                if c >= 1:
                    m3(pe, c - 1, (c - 1) % 2)


def kernel(x, src, dst, edge_attr_32, L0_gnn_mW1, L0_gnn_mb1, L0_gnn_mW2, L0_gnn_mb2,
           L0_gnn_uW1, L0_gnn_ub1, L0_gnn_uW2, L0_gnn_ub2):
    import numpy as np
    import concourse.bacc as bacc
    from concourse.bass_utils import run_bass_kernel_spmd

    x, src, dst, edge = (np.asarray(a) for a in (x, src, dst, edge_attr_32))
    pad = EDGES - N_EDGES
    src_p = np.concatenate([src, np.zeros(pad, src.dtype)])
    dst_p = np.concatenate([dst, np.full(pad, N_NODES, dst.dtype)])
    edge_p = np.concatenate([edge, np.zeros((pad, DE), edge.dtype)])
    x_p = np.concatenate([x, np.zeros((NODES - N_NODES, D), x.dtype)])
    src_tiles = np.ascontiguousarray(src_p.reshape(TILES, P).T)
    arrays = {
        "x_rows": x,
        "x_t": np.ascontiguousarray(x_p.T),
        "src_first": np.ascontiguousarray(src_tiles[:, :UNROLL * TPG]),
        "src_all": src_tiles,
        "dst_groups": dst_p.reshape(GROWS, GPP * GE),
        "dst_tiles": np.ascontiguousarray(dst_p.reshape(TILES, P).T),
        "edge_t": np.ascontiguousarray(edge_p.T),
        "mw1": np.asarray(L0_gnn_mW1), "mb1": np.asarray(L0_gnn_mb1),
        "mw2": np.asarray(L0_gnn_mW2), "mb2": np.asarray(L0_gnn_mb2),
        "uw1": np.asarray(L0_gnn_uW1), "ub1": np.asarray(L0_gnn_ub1),
        "uw2": np.asarray(L0_gnn_uW2), "ub2": np.asarray(L0_gnn_ub2),
    }
    nc = bacc.Bacc("TRN2", target_bir_lowering=False, num_devices=1)
    args = [nc.dram_tensor(name, a.shape, mybir.dt.from_np(a.dtype), kind="ExternalInput").ap()
            for name, a in arrays.items()]
    out = nc.dram_tensor("out", (N_NODES, D), mybir.dt.float32, kind="ExternalOutput").ap()
    build(nc, *args, out)
    return run_bass_kernel_spmd(nc, [arrays], core_ids=[0]).results[0]["out"]
```

```python
import concourse.bass as bass
from concourse import mybir
from contextlib import ExitStack

N_NODES = 12500
N_EDGES = 200000
D = 64
DE = 32
DH = 128
P = 128

TPG = 4
GE = TPG * P
UNROLL = 8
GROUPS = -(-N_EDGES // (GE * UNROLL)) * UNROLL
ITERS = GROUPS // UNROLL
EDGES = GROUPS * GE
TILES = GROUPS * TPG
GPP = 4
GROWS = GROUPS // GPP
G_END = -(-N_EDGES // GE)
T_END = -(-N_EDGES // P)
WIN = 96
BLOCKS = -(-N_NODES // P)
NODES = BLOCKS * P
LAST_BASE = NODES - WIN
RING = 4
KX = D + DE + 1
TRASH = NODES
AGG_ROWS = NODES + P
AGG_W = DH + 1
CB = 7
CHUNKS = BLOCKS // CB
CN = CB * P
CW = CB * D
HALF = CN // 2
UPD_LAP = ITERS - CHUNKS + 1
TB = 4
TSTEPS = -(-BLOCKS // TB)
TSLOTS = 5
EPS = 1e-5
assert EDGES == TILES * P and GROWS * GPP == GROUPS and CHUNKS * CB == BLOCKS
assert (ITERS - 1) * UNROLL < G_END <= GROUPS and 2 * GPP == UNROLL and TSTEPS % TSLOTS == 0


def build(nc, x_rows, x_t, src_first, src_all, dst_groups, dst_tiles, edge_t,
          mw1, mb1, mw2, mb2, uw1, ub1, uw2, ub2, out):
    f32 = mybir.dt.float32
    i32 = mybir.dt.int32
    bf16 = mybir.dt.bfloat16
    ALU = mybir.AluOpType
    ACT = mybir.ActivationFunctionType
    X = mybir.AxisListType.X
    ds = bass.ds
    ET = mybir.EngineType

    ctx = ExitStack()
    with ctx:
        def sb(name, shape, dt=f32):
            return ctx.enter_context(nc.sbuf_tensor(name, shape, dt))

        def sem(name):
            return ctx.enter_context(nc.semaphore(name))

        def dram(name, shape, dt=f32):
            return nc.dram_tensor(name, shape, dt, kind="Internal").ap()

        table = dram("dst_table", (NODES, DH))
        base_i_dram = dram("window_base_i", (GROUPS,), i32)
        base_f_dram = dram("window_base_f", (GROUPS,))
        spread_dram = dram("window_spread", (GROUPS,))
        lag_dram = dram("window_lag", (GROUPS,))
        agg_dram = dram("agg_rows", (AGG_ROWS, AGG_W))

        ident = sb("ident", [P, P])
        iota_i = sb("iota_i", [P, WIN], i32)
        iota = sb("iota", [P, WIN])
        ones_bf = sb("ones_bf", [P, P], bf16)
        eps = sb("eps", [P, 1])
        w_xe = sb("w_xe", [KX, DH])
        w_dst = sb("w_dst", [D, DH])
        w2_pad = sb("w2_pad", [DH, P])
        b2_col = sb("b2_col", [P, 1])
        u1 = sb("u1", [2 * D, DH])
        c1_col = sb("c1_col", [DH, 1])
        u2 = sb("u2", [DH, D])
        c2_rows = sb("c2_rows", [P, D])

        agg_t = sb("agg_t", [DH, NODES])
        xc = sb("xc", [P, NODES])
        resid = sb("resid", [P, BLOCKS * D])

        src_idx = sb("src_idx", [P, TILES + TPG], i32)
        slot_idx = sb("slot_idx", [P, UNROLL * TPG], i32)
        dst_i = sb("dst_i", [P, TILES], i32)
        rel = sb("rel", [P, TILES])
        base_row = sb("base_row", [1, GROUPS], i32)
        spread_row = sb("spread_row", [1, GROUPS])
        lag_row = sb("lag_row", [1, GROUPS])
        path = sb("path", [1, 2], i32)
        lag_i = sb("lag_i", [GROWS, 1], i32)
        lag_f = sb("lag_f", [GROWS, 1])
        lag = sb("lag", [GROWS, GPP])
        base_mn = sb("base_mn", [GROWS, GPP])
        base_f = sb("base_f", [GROWS, GPP])
        base_i = sb("base_i", [GROWS, GPP], i32)
        dst_mx = sb("dst_mx", [GROWS, GPP])
        spread = sb("spread", [GROWS, GPP])

        xg = sb("xg", [P, UNROLL, TPG * D])
        xe = sb("xe", [KX, RING, GE])
        win_tab = sb("win_tab", [WIN, RING, DH])
        oh = sb("oh", [P, RING, TPG * WIN])
        oh_t = sb("oh_t", [WIN, 2, GE])
        hid = sb("hid", [P, 2, TPG * DH])

        dst_g = resid[0:GROWS, 0:GPP * GE].bitcast(i32)
        dst_g_real = resid[0:GROWS, GPP * GE:2 * GPP * GE]
        base_all = resid[:, 2 * GPP * GE:2 * GPP * GE + GROUPS]
        tab_out = [hid[:, 0, :], hid[:, 1, :]] + [resid[:, BLOCKS * D - (n + 1) * TB * DH:][:, 0:TB * DH]
                                                  for n in range(TSLOTS - 2)]
        upd_h = dst_i[:, 0:CN].bitcast(f32)
        upd_sq = dst_i[:, CN:CN + CW].bitcast(f32)

        banks = [ctx.enter_context(nc.psum_tensor(f"bank{i}", [P, 512], f32)) for i in range(8)]
        ps_x, ps_h, ps_a, ps_o = banks[0:2], banks[2:4], banks[4:6], banks[6]

        s_first = sem("s_first")
        s_src = sem("s_src")
        s_dstg = sem("s_dstg")
        s_dstt = sem("s_dstt")
        s_wmsg = sem("s_wmsg")
        s_wdst = sem("s_wdst")
        s_wupd = sem("s_wupd")
        s_xt = [sem(f"s_xt{n}") for n in range(4)]
        s_const = sem("s_const")
        s_iota = sem("s_iota")
        s_ident = sem("s_ident")
        s_iotaf = sem("s_iotaf")
        s_zero_dve = sem("s_zero_dve")
        s_zero_act = sem("s_zero_act")
        s_zero_w2 = sem("s_zero_w2")
        s_one_row = sem("s_one_row")
        s_win = sem("s_win")
        s_base = sem("s_base")
        s_scratch = sem("s_scratch")
        s_back = sem("s_back")
        s_flag = sem("s_flag")
        s_rel = sem("s_rel")
        s_lag = sem("s_lag")
        s_tab_mm = sem("s_tab_mm")
        s_tab_cp = sem("s_tab_cp")
        s_tab_st = [sem(f"s_tab_st{n}") for n in range(TSLOTS)]
        s_gathered = [sem(f"s_gathered{i}") for i in range(UNROLL)]
        s_edge = [sem(f"s_edge{i}") for i in range(RING)]
        s_wtab = [sem(f"s_wtab{i}") for i in range(RING)]
        s_idx = sem("s_idx")
        s_opened = sem("s_opened")
        s_xt_mm = sem("s_xt_mm")
        s_xe = sem("s_xe")
        s_oh = sem("s_oh")
        s_oht_mm = sem("s_oht_mm")
        s_oht = sem("s_oht")
        s_h = sem("s_h")
        s_relu = sem("s_relu")
        s_agg = sem("s_agg")
        s_added = sem("s_added")
        s_c2 = sem("s_c2")
        s_m1 = sem("s_m1")
        s_u = sem("s_u")
        s_m2 = sem("s_m2")
        s_hu = sem("s_hu")
        s_m3 = sem("s_m3")
        s_sum = sem("s_sum")
        s_summed = sem("s_summed")
        s_mean = sem("s_mean")
        s_red = sem("s_red")
        s_dev = sem("s_dev")
        s_sq = sem("s_sq")
        s_var = sem("s_var")
        s_std = sem("s_std")
        s_rstd = sem("s_rstd")
        s_norm = sem("s_norm")
        s_out = sem("s_out")

        def wait(eng, s, n):
            if not isinstance(n, int) or n > 0:
                eng.wait_ge(s, n)

        def gather(pool, g, k, tiles=TPG):
            wait(pool, s_idx, g - UNROLL + 1)
            pool.sem_inc(s_opened, 1)
            for j in range(tiles):
                c = k * TPG + j
                pool.indirect_dma_start(
                    out=xg[:, k, j * D:(j + 1) * D], out_offset=None, in_=x_rows,
                    in_offset=bass.IndirectOffsetOnAxis(ap=slot_idx[:, c:c + 1], axis=0),
                ).then_inc(s_gathered[k], 16)

        def load_operands(sp, g, k, base):
            r = k % RING
            wait(sp, s_h, g - RING + 1)
            sp.dma_start(xe[D:D + DE, r, :], edge_t[:, ds(g * GE, GE)]).then_inc(s_edge[r], 16)
            sp.dma_start(win_tab[:, r, :], table[ds(base, WIN), :]).then_inc(s_wtab[r], 16)

        def transpose_x(pe, g, k, lap):
            q = k % 2
            missing = G_END * TPG - T_END if isinstance(g, int) and g == G_END - 1 else 0
            wait(pe, s_gathered[k], (lap + 1) * 16 * TPG - 16 * missing)
            wait(pe, s_xe, g - 1)
            for m in range(TPG // 2):
                last = nc.tensor.transpose(ps_x[q][:, m * P:(m + 1) * P],
                                           xg[:, k, m * 2 * D:(m + 1) * 2 * D], ident[:, :])
            last.then_inc(s_xt_mm, 1)

        def transpose_oh(pe, g, k):
            r = k % RING
            wait(pe, s_oh, g + 1)
            wait(pe, s_oht, g)
            for j in range(TPG):
                last = nc.tensor.transpose(ps_o[0:WIN, j * P:(j + 1) * P],
                                           oh[:, r, j * WIN:(j + 1) * WIN], ident[:, :])
            last.then_inc(s_oht_mm, 1)

        def hidden(pe, g, k, lap):
            q, r = k % 2, k % RING
            n = lap * (UNROLL // RING) + k // RING + 1
            wait(pe, s_xe, g + 1)
            wait(pe, s_edge[r], n * 16)
            wait(pe, s_wtab[r], n * 16)
            wait(pe, s_oht, g + 1)
            wait(pe, s_relu, g - 1)
            for j in range(TPG):
                o = ps_h[q][:, j * DH:(j + 1) * DH]
                nc.tensor.matmul(o, xe[:, r, j * P:(j + 1) * P], w_xe[:, :], start=True, stop=False)
                last = nc.tensor.matmul(o, oh_t[:, q, j * P:(j + 1) * P], win_tab[:, r, :],
                                        start=False, stop=True)
            last.then_inc(s_h, 1)

        def aggregate(pe, g, k):
            q, r = k % 2, k % RING
            wait(pe, s_relu, g + 1)
            wait(pe, s_added, g - 1)
            for j in range(TPG):
                nc.tensor.matmul(ps_a[q][:, 0:WIN], hid[:, q, j * DH:(j + 1) * DH],
                                 oh[:, r, j * WIN:(j + 1) * WIN], start=(j == 0), stop=(j == TPG - 1))
            half = oh[:, r, :].bitcast(bf16).rearrange("p (n two) -> p n two", two=2)
            for j in range(TPG):
                last = nc.tensor.matmul(ps_a[q][:, WIN:2 * WIN], ones_bf[:, :],
                                        half[:, j * WIN:(j + 1) * WIN, 1],
                                        start=(j == 0), stop=(j == TPG - 1))
            last.then_inc(s_agg, 1)

        def copy_x(g, k):
            act = nc.scalar
            q, r = k % 2, k % RING
            wait(act, s_xt_mm, g + 1)
            wait(act, s_h, g - RING + 1)
            to = xe[0:D, r, :].rearrange("p (m t e) -> p m t e", t=2, e=P)
            for t in range(2):
                of = ps_x[q][t * D:(t + 1) * D, 0:GE // 2].rearrange("p (m e) -> p m e", e=P)
                last = act.activation(to[:, :, t, :], of, ACT.Copy)
            last.then_inc(s_xe, 1)

        def relu(g, k):
            act = nc.scalar
            q = k % 2
            wait(act, s_h, g + 1)
            wait(act, s_agg, g - 1)
            act.activation(hid[:, q, :], ps_h[q][:, :], ACT.Relu).then_inc(s_relu, 1)

        def one_hot(g, k):
            dve = nc.vector
            r = k % RING
            wait(dve, s_agg, g - RING + 1)
            grid = [P, TPG, WIN]
            dve.tensor_tensor(oh[:, r, :].rearrange("p (j w) -> p j w", w=WIN),
                              iota[:, None, :].to_broadcast(grid),
                              rel[:, ds(g * TPG, TPG)][:, :, None].to_broadcast(grid),
                              ALU.is_equal).then_inc(s_oh, 1)

        def copy_oh(g, k):
            dve = nc.vector
            q = k % 2
            wait(dve, s_oht_mm, g + 1)
            wait(dve, s_h, g - 1)
            dve.tensor_copy(oh_t[:, q, :], ps_o[0:WIN, :]).then_inc(s_oht, 1)

        def next_indices(g, k):
            dve = nc.vector
            wait(dve, s_xt_mm, g + 1)
            dve.tensor_copy(slot_idx[:, k * TPG:(k + 1) * TPG],
                            src_idx[:, ds((g + UNROLL) * TPG, TPG)]).then_inc(s_idx, 1)

        def add_window(g, k, base):
            dve = nc.vector
            q = k % 2
            wait(dve, s_agg, g + 1)
            wait(dve, s_added, g)
            to, cnt = agg_t[:, ds(base, WIN)], xc[D:P, ds(base, WIN)]
            dve.tensor_tensor(to, ps_a[q][:, 0:WIN], to, ALU.add)
            dve.tensor_tensor(cnt, ps_a[q][D:P, WIN:2 * WIN], cnt, ALU.add).then_inc(s_added, 1)

        def window_bases(eng, start, n):
            return nc.values_load_multi_w_load_instructions(
                base_row[0:1, ds(start, n)], engines=(eng,), min_val=0, max_val=LAST_BASE,
                skip_runtime_bounds_check_because="the chip clamps them to this range")[1]

        quarters = [n * TB * P for n in (0, 3, 9, 16)] + [NODES]

        def table_stored(eng):
            for n in range(TSLOTS):
                eng.wait_ge(s_tab_st[n], TSTEPS // TSLOTS * 16)

        def laps(eng, lap, open_update, chunk):
            lap(0, None)
            with eng.Fori(1, UPD_LAP) as i:
                lap(i, None)
            open_update()
            behind = eng.value_load(path[0:1, 1:2], min_val=0, max_val=NODES)
            with eng.If(behind < 1):
                with eng.Fori(UPD_LAP, ITERS - 1) as i:
                    lap(i, i - UPD_LAP)
                lap(ITERS - 1, CHUNKS - 2)
                chunk(CHUNKS - 1)
            with eng.Else():
                with eng.Fori(UPD_LAP, ITERS - 1) as i:
                    lap(i, None)
                lap(ITERS - 1, None)
                all_chunks(eng, chunk)

        def all_chunks(eng, chunk):
            with eng.Fori(0, CHUNKS - 1) as c:
                chunk(c)
            chunk(CHUNKS - 1)

        def exists(g):
            return not isinstance(g, int) or g < G_END

        def windows_fit(eng, body, other):
            eng.wait_ge(s_flag, 2)
            widest = eng.value_load(path[0:1, 0:1], min_val=0, max_val=NODES)
            with eng.If(widest < WIN):
                body()
            with eng.Else():
                other()

        g_x = xg[:, 0, 0:P]
        g_tab = hid[:, 0, 0:DH]
        g_dcol = rel[:, 0:1]
        g_dbc = hid[:, 0, DH:2 * DH]
        g_same = hid[:, 0, 2 * DH:3 * DH]
        g_low = hid[:, 0, 3 * DH:4 * DH]
        g_pre = hid[:, 1, 0:DH]
        g_h = oh[:, 0, 0:AGG_W]
        g_sum = oh[:, 1, 0:AGG_W]
        g_earlier = hid[:, 1, 2 * DH:3 * DH]
        g_scr = rel[:, 8:16]
        g_xe = xe[:, 0, 0:P]
        g_back = oh[:, 2, 0:AGG_W]
        g_cbc = hid[:, 1, 3 * DH:4 * DH]
        g_si, g_di, g_to = slot_idx[:, 0:1], slot_idx[:, 1:2], slot_idx[:, 2:3]
        t_zero = sem("t_zero")
        t_init = sem("t_init")
        t_low = sem("t_low")
        t_gat = sem("t_gat")
        t_edge = sem("t_edge")
        t_tr = sem("t_tr")
        t_xe = sem("t_xe")
        t_h = sem("t_h")
        t_same = sem("t_same")
        t_pre = sem("t_pre")
        t_relu = sem("t_relu")
        t_sum = sem("t_sum")
        t_step = sem("t_step")
        t_out = sem("t_out")
        t_scat = sem("t_scat")
        t_rows = sem("t_rows")
        t_cbc = sem("t_cbc")
        t_btr = sem("t_btr")
        t_bcp = sem("t_bcp")
        DVE_STEPS = 4

        def general_pool():
            pool = nc.gpsimd
            for k in range(UNROLL):
                pool.wait_ge(s_gathered[k], 16 * TPG)
            table_stored(pool)
            pool.memset(g_x[:, D:P], 0.0).then_inc(t_zero, 1)
            pool.memset(g_low, 1.0).then_inc(t_low, 1)
            pool.wait_ge(t_low, 1)
            pool.affine_select(out=g_low, in_=g_low, compare_op=ALU.is_gt, fill=0.0, base=0,
                               pattern=[[-1, P]], channel_multiplier=1).then_inc(t_low, 1)
            with pool.Fori(0, T_END) as t:
                pool.wait_ge(t_step, t * DVE_STEPS + 1)
                pool.sem_inc(s_opened, 1)
                pool.indirect_dma_start(
                    out=g_x[:, 0:D], out_offset=None, in_=x_rows,
                    in_offset=bass.IndirectOffsetOnAxis(ap=g_si, axis=0)).then_inc(t_gat, 16)
                pool.indirect_dma_start(
                    out=g_tab, out_offset=None, in_=table,
                    in_offset=bass.IndirectOffsetOnAxis(ap=g_di, axis=0)).then_inc(t_gat, 16)
                pool.wait_ge(t_out, t + 1)
                pool.sem_inc(s_opened, 1)
                pool.indirect_dma_start(
                    out=agg_dram, out_offset=bass.IndirectOffsetOnAxis(ap=g_to, axis=0),
                    in_=g_sum, in_offset=None, compute_op=ALU.add).then_inc(t_scat, 16)

        def general_sync():
            sp = nc.sync
            half = AGG_ROWS * AGG_W // P // 2
            rows = agg_dram.rearrange("(p r) w -> p (r w)", p=P)
            sp.wait_ge(s_zero_act, 1)
            at = 0
            for n in (half, rows.shape[1] - half):
                sp.dma_start(rows[:, at:at + n], agg_t[:, 0:n]).then_inc(t_init, 16)
                at += n
            with sp.Fori(0, T_END) as t:
                sp.wait_ge(t_step, t * DVE_STEPS + 1)
                sp.dma_start(g_xe[D:D + DE, :], edge_t[:, ds(t * P, P)]).then_inc(t_edge, 16)
            sp.wait_ge(t_scat, T_END * 16)
            with sp.Fori(0, BLOCKS) as b:
                sp.wait_ge(t_bcp, b + 1)
                sp.dma_start(g_back, agg_dram[ds(b * P, P), :]).then_inc(t_rows, 16)

        def general_tensor():
            pe = nc.tensor
            pe.wait_ge(t_zero, 1)
            with pe.Fori(0, T_END) as t:
                pe.wait_ge(t_gat, (t + 1) * 32)
                pe.wait_ge(t_step, t * DVE_STEPS + 2)
                nc.tensor.transpose(ps_x[0][:, 0:P], g_x, ident[:, :])
                nc.tensor.transpose(ps_o[:, 0:P], g_dbc, ident[:, :]).then_inc(t_tr, 1)
                pe.wait_ge(t_xe, t + 1)
                pe.wait_ge(t_edge, (t + 1) * 16)
                nc.tensor.matmul(ps_h[0][:, 0:DH], g_xe, w_xe[:, :],
                                 start=True, stop=True).then_inc(t_h, 1)
                pe.wait_ge(t_same, t + 1)
                pe.wait_ge(t_relu, t + 1)
                nc.tensor.matmul(ps_a[0][:, 0:AGG_W], g_same, g_h,
                                 start=True, stop=True).then_inc(t_sum, 1)
            with pe.Fori(0, BLOCKS) as b:
                pe.wait_ge(t_cbc, b + 1)
                nc.tensor.transpose(ps_x[0][:, 0:P], g_back[:, 0:DH], ident[:, :])
                nc.tensor.transpose(ps_o[:, 0:P], g_cbc, ident[:, :]).then_inc(t_btr, 1)

        def general_scalar():
            act = nc.scalar
            with act.Fori(0, T_END) as t:
                act.wait_ge(t_tr, t + 1)
                act.activation(g_xe[0:D, :], ps_x[0][0:D, 0:P], ACT.Copy).then_inc(t_xe, 1)
                act.wait_ge(t_pre, t + 1)
                act.activation(g_h[:, 0:DH], g_pre, ACT.Relu).then_inc(t_relu, 1)

        def general_vector():
            dve = nc.vector
            table_stored(dve)
            dve.wait_ge(s_src, 16)
            dve.wait_ge(t_low, 2)
            dve.wait_ge(t_init, 32)
            dve.memset(g_h[:, DH:AGG_W], 1.0).then_inc(t_bcp, 1)
            dve.wait_ge(t_bcp, 1)
            with dve.Fori(0, T_END) as t:
                at = t * DVE_STEPS
                dve.tensor_copy(g_si, src_idx[:, ds(t, 1)])
                dve.tensor_copy(g_dcol, dst_i[:, ds(t, 1)])
                dve.tensor_copy(g_di, dst_i[:, ds(t, 1)]).then_inc(t_step, 1)
                dve.wait_ge(t_step, at + 1)
                dve.tensor_copy(g_dbc, g_dcol.to_broadcast([P, P])).then_inc(t_step, 1)
                dve.wait_ge(t_tr, t + 1)
                dve.tensor_scalar(g_same, ps_o[:, 0:P], g_dcol, None, ALU.is_equal).then_inc(t_same, 1)
                dve.wait_ge(t_h, t + 1)
                dve.tensor_tensor(g_pre, ps_h[0][:, 0:DH], g_tab, ALU.add).then_inc(t_pre, 1)
                dve.wait_ge(t_same, t + 1)
                dve.tensor_tensor(g_earlier, g_same, g_low, ALU.mult).then_inc(t_step, 1)
                dve.wait_ge(t_step, at + 3)
                dve.reduce_max(g_scr[:, 0:1], g_earlier, X).then_inc(t_step, 1)
                dve.wait_ge(t_step, at + 4)
                general_row(dve, t)
                dve.wait_ge(t_sum, t + 1)
                dve.tensor_copy(g_sum, ps_a[0][:, 0:AGG_W]).then_inc(t_out, 1)
                dve.wait_ge(t_scat, (t + 1) * 16)

            with dve.Fori(0, BLOCKS) as b:
                dve.wait_ge(t_rows, (b + 1) * 16)
                dve.tensor_copy(g_cbc, g_back[:, DH:AGG_W].to_broadcast([P, P])).then_inc(t_cbc, 1)
                dve.wait_ge(t_btr, b + 1)
                dve.tensor_copy(agg_t[:, ds(b * P, P)], ps_x[0][:, 0:P])
                dve.tensor_copy(xc[D:P, ds(b * P, P)], ps_o[D:P, 0:P]).then_inc(t_bcp, 1)
            dve.wait_ge(t_bcp, BLOCKS + 1)

        t_row = sem("t_row")
        trash_f = sb("trash_f", [P, 1])
        trash_i = sb("trash_i", [P, 1], i32)

        def general_row(dve, t):
            dve.tensor_tensor(g_scr[:, 1:2], trash_f[:, :], g_dcol, ALU.subtract).then_inc(t_row, 1)
            dve.wait_ge(t_row, t * 2 + 1)
            dve.tensor_tensor(g_scr[:, 2:3], g_scr[:, 1:2], g_scr[:, 0:1], ALU.mult).then_inc(t_row, 1)
            dve.wait_ge(t_row, t * 2 + 2)
            dve.tensor_tensor(g_to, g_scr[:, 2:3], g_dcol, ALU.add)

        stat = sb("stat", [P, 4 * CB])
        st_sum, st_mean, st_var, st_std = (stat[:, n * CB:(n + 1) * CB] for n in range(4))
        st_rstd = st_sum

        def half_of(t, c, h):
            return t[:, ds(c * CN + h * HALF, HALF)]

        def rows_of(c):
            return resid[:, ds(c * CW, CW)]

        def blocks(ap):
            return ap.rearrange("p (b d) -> p b d", d=D)

        def bank_of(alone, n):
            return banks[n] if alone else banks[7]

        def pe_m1(c, h, alone):
            pe = nc.tensor
            if h == 0:
                pe.wait_ge(s_c2, c + 1)
            elif not alone:
                pe.wait_ge(s_u, c * 2 + 1)
            nc.tensor.matmul(bank_of(alone, h)[:, 0:HALF], w2_pad[:, :], half_of(agg_t, c, h),
                             start=True, stop=True).then_inc(s_m1, 1)

        def pe_m2(c, h, alone):
            pe = nc.tensor
            pe.wait_ge(s_u, c * 2 + (1 + h if alone else 2))
            if h == 1 and not alone:
                pe.wait_ge(s_hu, c * 2 + 1)
            nc.tensor.matmul(bank_of(alone, 2 + h)[:, 0:HALF], u1[:, :], half_of(xc, c, h),
                             start=True, stop=True).then_inc(s_m2, 1)

        def pe_m3(c, alone):
            pe = nc.tensor
            pe.wait_ge(s_hu, c * 2 + 2)
            for b in range(CB):
                last = nc.tensor.matmul(bank_of(alone, 4)[:, b * D:(b + 1) * D],
                                        upd_h[:, b * P:(b + 1) * P], u2[:, :], start=True, stop=True)
            last.then_inc(s_m3, 1)

        def dve_c2(c):
            y = blocks(rows_of(c))
            nc.vector.tensor_tensor(y, y, c2_rows[:, None, :].to_broadcast([P, CB, D]), ALU.add
                                    ).then_inc(s_c2, 1)

        def dve_stack(c, h, alone):
            dve = nc.vector
            dve.wait_ge(s_m1, c * 2 + h + 1)
            cnt = xc[D:P, ds(c * CN + h * HALF, HALF)]
            dve.scalar_tensor_tensor(cnt, cnt, b2_col[D:P, 0:1], bank_of(alone, h)[D:P, 0:HALF],
                                     ALU.mult, ALU.add).then_inc(s_u, 1)

        def act_relu(c, h, alone):
            act = nc.scalar
            act.wait_ge(s_m2, c * 2 + h + 1)
            act.activation(upd_h[:, h * HALF:(h + 1) * HALF], bank_of(alone, 2 + h)[:, 0:HALF], ACT.Relu,
                           bias=c1_col[:, 0:1]).then_inc(s_hu, 1)

        def dve_center(c, alone):
            dve = nc.vector
            y = rows_of(c)
            dve.wait_ge(s_m3, c + 1)
            dve.tensor_tensor(y, bank_of(alone, 4)[:, 0:CW], y, ALU.add).then_inc(s_sum, 1)
            dve.wait_ge(s_sum, c + 1)
            dve.sem_inc(s_summed, 1)
            dve.reduce_sum(st_sum, blocks(y), X).then_inc(s_red, 1)
            dve.wait_ge(s_red, c + 1)
            dve.tensor_scalar(st_mean, st_sum, 1.0 / D, None, ALU.mult).then_inc(s_mean, 1)
            dve.wait_ge(s_mean, c + 1)
            dve.tensor_tensor(blocks(y), blocks(y), st_mean[:, :, None].to_broadcast([P, CB, D]),
                              ALU.subtract).then_inc(s_dev, 1)

        def act_square(c):
            act = nc.scalar
            act.wait_ge(s_dev, c + 1)
            act.activation(upd_sq, rows_of(c), ACT.Square).then_inc(s_sq, 1)

        def dve_variance(c):
            dve = nc.vector
            dve.wait_ge(s_sq, c + 1)
            dve.reduce_sum(st_var, blocks(upd_sq), X).then_inc(s_var, 1)

        def act_deviation(c):
            act = nc.scalar
            act.wait_ge(s_var, c + 1)
            act.activation(st_std, st_var, ACT.Sqrt, bias=eps[:, 0:1], scale=1.0 / D).then_inc(s_std, 1)

        def dve_normalize(c):
            dve = nc.vector
            y = blocks(rows_of(c))
            dve.wait_ge(s_std, c + 1)
            dve.reciprocal(st_rstd, st_std).then_inc(s_rstd, 1)
            dve.wait_ge(s_rstd, c + 1)
            dve.tensor_tensor(y, y, st_rstd[:, :, None].to_broadcast([P, CB, D]), ALU.mult
                              ).then_inc(s_norm, 1)

        def act_store(c):
            act = nc.scalar
            act.wait_ge(s_norm, c + 1)
            if isinstance(c, int) and c == CHUNKS - 1:
                whole, rest = divmod(N_NODES - c * CN, P)
                act.dma_start(out[c * CN + whole * P:, :],
                              rows_of(c)[0:rest, whole * D:(whole + 1) * D]).then_inc(s_out, 16)
            else:
                whole = CB
            act.dma_start(out[ds(c * CN, whole * P), :].rearrange("(b p) d -> p b d", p=P),
                          blocks(rows_of(c))[:, 0:whole, :]).then_inc(s_out, 16)

        def pe_chunk(c):
            for h in range(2):
                pe_m1(c, h, True)
            for h in range(2):
                pe_m2(c, h, True)
            pe_m3(c, True)

        def act_chunk(c):
            for h in range(2):
                act_relu(c, h, True)
            act_square(c)
            act_deviation(c)
            act_store(c)

        def dve_chunk(c):
            dve_c2(c)
            for h in range(2):
                dve_stack(c, h, True)
            dve_center(c, True)
            dve_variance(c)
            dve_normalize(c)

        block = ctx.enter_context(nc.Block())

        @block.gpsimd
        def _(pool):
            pool.iota(iota_i[:, :], pattern=[[1, WIN]], base=0, channel_multiplier=0).then_inc(s_iota, 1)
            pool.memset(ident[:, :], 0.0).then_inc(s_ident, 1)
            pool.wait_ge(s_ident, 1)
            pool.affine_select(out=ident[:, :], in_=ident[:, :], compare_op=ALU.not_equal, fill=1.0,
                               base=0, pattern=[[-1, P]], channel_multiplier=1).then_inc(s_ident, 1)
            pool.iota(trash_i[:, :], pattern=[[0, 1]], base=TRASH, channel_multiplier=1).then_inc(s_iota, 1)
            pool.iota(lag_i[:, :], pattern=[[0, 1]], base=(1 - UPD_LAP) * CN, channel_multiplier=CN // 2
                      ).then_inc(s_iota, 1)
            pool.wait_ge(s_first, 16)
            for k in range(UNROLL):
                gather(pool, k, k)

            def windowed():
                with pool.Fori(1, ITERS - 1) as i:
                    for k in range(UNROLL):
                        gather(pool, i * UNROLL + k, k)
                for g in range((ITERS - 1) * UNROLL, G_END):
                    gather(pool, g, g % UNROLL, min(TPG, T_END - g * TPG))

            windows_fit(pool, windowed, general_pool)

        @block.sync
        def _(sp):
            sp.dma_start(slot_idx[:, :], src_first).then_inc(s_first, 16)
            sp.dma_start(dst_g, dst_groups).then_inc(s_dstg, 16)
            sp.dma_start(w_xe[0:D, :], mw1[0:D, :]).then_inc(s_wmsg, 16)
            sp.dma_start(w_xe[D:D + DE, :], mw1[2 * D:2 * D + DE, :]).then_inc(s_wmsg, 16)
            sp.dma_start(w_xe[D + DE:KX, :], mb1[None, :]).then_inc(s_wmsg, 16)
            sp.wait_ge(s_win, 5)
            for to, of in ((base_f_dram, base_f), (spread_dram, spread), (lag_dram, lag), (base_i_dram, base_i)):
                sp.dma_start(to.rearrange("(p g) -> p g", g=GPP), of[:, :]).then_inc(s_scratch, 16)
            sp.wait_ge(s_scratch, 64)
            sp.dma_start(base_all, base_f_dram[None, :].to_broadcast([P, GROUPS])).then_inc(s_back, 16)
            sp.dma_start(spread_row[:, :], spread_dram[None, :]).then_inc(s_back, 16)
            sp.dma_start(lag_row[:, :], lag_dram[None, :]).then_inc(s_back, 16)
            sp.dma_start(base_row[:, :], base_i_dram[None, :]).then_inc(s_back, 16)
            sp.dma_start(src_idx[:, 0:TILES], src_all).then_inc(s_src, 16)
            table_stored(sp)
            sp.wait_ge(s_back, 64)

            def load_update():
                main = BLOCKS - 1
                sp.wait_ge(s_zero_w2, 1)
                sp.dma_start(w2_pad[:, D:P], mw2).then_inc(s_wupd, 16)
                sp.dma_start(b2_col[D:P, :], mb2[:, None]).then_inc(s_wupd, 16)
                sp.dma_start(u1[:, :], uw1).then_inc(s_wupd, 16)
                sp.dma_start(c1_col[:, :], ub1[:, None]).then_inc(s_wupd, 16)
                sp.dma_start(u2[:, :], uw2).then_inc(s_wupd, 16)
                sp.dma_start(c2_rows[:, :], ub2[None, :].to_broadcast([P, D])).then_inc(s_wupd, 16)
                sp.wait_ge(s_flag, 2)
                sp.dma_start(resid[:, 0:main * D].rearrange("p (b d) -> p b d", d=D),
                             x_rows[0:main * P, :].rearrange("(b p) d -> p b d", p=P)
                             ).then_inc(s_wupd, 16)
                sp.dma_start(resid[0:N_NODES - main * P, main * D:], x_rows[main * P:, :]
                             ).then_inc(s_wupd, 16)

            def windowed():
                def lap(i, c=None):
                    bases = window_bases(ET.SP, i * UNROLL, UNROLL)
                    for k in range(UNROLL):
                        if exists(i * UNROLL + k):
                            load_operands(sp, i * UNROLL + k, k, bases[k])
                lap(0)
                load_update()
                with sp.Fori(1, ITERS - 1) as i:
                    lap(i)
                lap(ITERS - 1)

            def general():
                load_update()
                general_sync()

            windows_fit(sp, windowed, general)

        @block.scalar
        def _(act):
            act.dma_start(w_dst[:, :], mw1[D:2 * D, :]).then_inc(s_wdst, 16)
            for n in range(4):
                part = slice(quarters[n], quarters[n + 1])
                act.dma_start(xc[0:D, part], x_t[:, part]).then_inc(s_xt[n], 16)
            act.dma_start(dst_i[:, :], dst_tiles).then_inc(s_dstt, 16)
            act.memzero(agg_t[:, :]).then_inc(s_zero_act, 1)
            for n in range(TSTEPS + 1):
                if n < TSTEPS:
                    w = min(TB, BLOCKS - n * TB) * DH
                    act.wait_ge(s_tab_mm, n + 1)
                    if n >= TSLOTS:
                        act.wait_ge(s_tab_st[n % TSLOTS], n // TSLOTS * 16)
                    if n == 2:
                        act.wait_ge(s_flag, 2)
                    act.activation(tab_out[n % TSLOTS][:, 0:w], banks[n % 4][:, 0:w],
                                   ACT.Copy).then_inc(s_tab_cp, 1)
                if n > 0:
                    act.wait_ge(s_tab_cp, n)
                    nb = min(TB, BLOCKS - (n - 1) * TB)
                    act.dma_start(table[(n - 1) * TB * P:((n - 1) * TB + nb) * P, :].rearrange(
                                      "(b p) n -> p b n", p=P),
                                  tab_out[(n - 1) % TSLOTS][:, 0:nb * DH].rearrange(
                                      "p (b n) -> p b n", n=DH)).then_inc(s_tab_st[(n - 1) % TSLOTS], 16)

            def open_update():
                act.wait_ge(s_wupd, 128)

            def windowed():
                table_stored(act)
                copy_x(0, 0)

                def lap(i, c):
                    for k in range(UNROLL):
                        g = i * UNROLL + k
                        if c is not None and k == 7:
                            act_square(c)
                        if exists(g + 1):
                            copy_x(g + 1, (k + 1) % UNROLL)
                        if c is not None and k == 7:
                            act_deviation(c)
                        if exists(g):
                            relu(g, k)
                        if c is not None and k in (4, 5):
                            act_relu(c, k - 4, False)
                        if c is not None and k == 7:
                            act_store(c)
                laps(act, lap, open_update, act_chunk)

            def general():
                open_update()
                general_scalar()
                all_chunks(act, act_chunk)

            windows_fit(act, windowed, general)
            act.wait_ge(s_out, (CHUNKS + 1) * 16)

        @block.vector
        def _(dve):
            dve.memset(ones_bf[:, :], 1.0)
            dve.memset(src_idx[:, TILES:], 0)
            dve.memset(eps[:, :], EPS).then_inc(s_const, 1)
            dve.memset(xe[D + DE:KX, :, :], 1.0).then_inc(s_one_row, 1)
            dve.wait_ge(s_iota, 3)
            dve.tensor_copy(iota[:, :], iota_i[:, :])
            dve.tensor_copy(trash_f[:, :], trash_i[:, :])
            dve.tensor_copy(lag_f[:, :], lag_i[:, :]).then_inc(s_iotaf, 1)
            dve.wait_ge(s_dstg, 16)
            dve.tensor_reduce(base_mn[:, :], dst_g.rearrange("p (g e) -> p g e", e=GE), X, ALU.min
                              ).then_inc(s_base, 1)
            dve.scalar_tensor_tensor(dst_g_real, dst_g, float(N_NODES), dst_g, ALU.is_lt, ALU.mult
                                     ).then_inc(s_base, 1)
            dve.wait_ge(s_base, 1)
            dve.tensor_scalar(base_f[:, :], base_mn[:, :], float(LAST_BASE), None, ALU.min
                              ).then_inc(s_win, 1)
            dve.wait_ge(s_base, 2)
            dve.reduce_max(dst_mx[:, :], dst_g_real.rearrange("p (g e) -> p g e", e=GE), X).then_inc(s_win, 1)
            dve.wait_ge(s_win, 2)
            dve.tensor_copy(base_i[:, :], base_f[:, :]).then_inc(s_win, 1)
            dve.tensor_tensor(spread[:, :], dst_mx[:, :], base_f[:, :], ALU.subtract).then_inc(s_win, 1)
            dve.wait_ge(s_iotaf, 1)
            dve.tensor_tensor(lag[:, :], lag_f[:, 0:1].to_broadcast([GROWS, GPP]), base_f[:, :],
                              ALU.subtract).then_inc(s_win, 1)
            dve.wait_ge(s_dstt, 16)
            dve.wait_ge(s_back, 64)
            grid = [P, GROUPS, TPG]
            dve.tensor_tensor(rel[:, :].rearrange("p (g j) -> p g j", j=TPG),
                              dst_i[:, :].rearrange("p (g j) -> p g j", j=TPG),
                              base_all[:, :, None].to_broadcast(grid), ALU.subtract).then_inc(s_rel, 1)
            dve.reduce_max(path[:, 0:1], spread_row[:, :], X).then_inc(s_flag, 1)
            dve.tensor_scalar(lag_row[:, :], lag_row[:, :], 0.0, None, ALU.max).then_inc(s_lag, 1)
            dve.wait_ge(s_lag, 1)
            dve.reduce_max(path[:, 1:2], lag_row[:, :], X).then_inc(s_flag, 1)
            dve.memset(xc[D:P, :], 0.0).then_inc(s_zero_dve, 1)
            dve.memset(w2_pad[:, 0:D], 0.0).then_inc(s_zero_w2, 1)

            def open_update():
                dve.wait_ge(s_wupd, 128)

            def windowed():
                dve.wait_ge(s_rel, 1)
                dve.wait_ge(s_src, 16)
                one_hot(0, 0)
                one_hot(1, 1)
                copy_oh(0, 0)
                next_indices(0, 0)
                dve.wait_ge(s_zero_act, 1)
                dve.wait_ge(s_zero_dve, 1)

                def lap(i, c):
                    if isinstance(i, int) and i == 0:
                        bases = [None, None, *window_bases(ET.DVE, 0, UNROLL - 2)]
                    else:
                        bases = window_bases(ET.DVE, i * UNROLL - 2, UNROLL)
                    for k in range(UNROLL):
                        g = i * UNROLL + k
                        if exists(g + 2):
                            one_hot(g + 2, (k + 2) % UNROLL)
                        if exists(g + 1):
                            copy_oh(g + 1, (k + 1) % UNROLL)
                        if exists(g + 1 + UNROLL):
                            next_indices(g + 1, (k + 1) % UNROLL)
                        if not (isinstance(g, int) and g < 2):
                            add_window(g - 2, (k - 2) % UNROLL, bases[k])
                        if c is not None:
                            if k == 1:
                                dve_c2(c)
                            elif k in (2, 3):
                                dve_stack(c, k - 2, False)
                            elif k == 6:
                                dve_center(c, False)
                            elif k == 7:
                                dve_variance(c)
                                dve_normalize(c)
                    if isinstance(i, int) and i == ITERS - 1:
                        last = ITERS * UNROLL - 2
                        for g, base in zip(range(last, G_END), window_bases(ET.DVE, last, 2)):
                            add_window(g, g % UNROLL, base)
                laps(dve, lap, open_update, dve_chunk)

            def general():
                open_update()
                general_vector()
                all_chunks(dve, dve_chunk)

            windows_fit(dve, windowed, general)

        @block.tensor
        def _(pe):
            pe.wait_ge(s_wdst, 16)
            for n in range(TSTEPS):
                for q in range(4):
                    if n * TB <= quarters[q] // P < (n + 1) * TB:
                        pe.wait_ge(s_xt[q], 16)
                wait(pe, s_tab_cp, n - 3)
                for b in range(min(TB, BLOCKS - n * TB)):
                    at = (n * TB + b) * P
                    last = nc.tensor.matmul(banks[n % 4][:, b * DH:(b + 1) * DH], xc[0:D, at:at + P],
                                            w_dst[:, :], start=True, stop=True)
                last.then_inc(s_tab_mm, 1)

            def open_update():
                pe.wait_ge(s_wupd, 128)

            def begin():
                pe.wait_ge(s_ident, 2)
                pe.wait_ge(s_tab_cp, TSTEPS)
                pe.wait_ge(s_wmsg, 48)
                pe.wait_ge(s_one_row, 1)
                pe.wait_ge(s_const, 1)

            def windowed():
                begin()
                transpose_x(pe, 0, 0, 0)
                transpose_oh(pe, 0, 0)

                def lap(i, c):
                    for k in range(UNROLL):
                        g = i * UNROLL + k
                        if c is not None:
                            if k in (2, 3):
                                pe_m1(c, k - 2, False)
                            elif k in (4, 5):
                                pe_m2(c, k - 4, False)
                            elif k == 6:
                                pe_m3(c, False)
                        if exists(g + 1):
                            transpose_x(pe, g + 1, (k + 1) % UNROLL, i + (k + 1) // UNROLL)
                            transpose_oh(pe, g + 1, (k + 1) % UNROLL)
                        if exists(g):
                            hidden(pe, g, k, i)
                        if not (isinstance(g, int) and (g == 0 or g > G_END)):
                            aggregate(pe, g - 1, (k - 1) % UNROLL)
                laps(pe, lap, open_update, pe_chunk)

            def general():
                begin()
                open_update()
                general_tensor()
                all_chunks(pe, pe_chunk)

            windows_fit(pe, windowed, general)


def kernel(x, src, dst, edge_attr_32, L0_gnn_mW1, L0_gnn_mb1, L0_gnn_mW2, L0_gnn_mb2,
           L0_gnn_uW1, L0_gnn_ub1, L0_gnn_uW2, L0_gnn_ub2):
    import numpy as np
    import concourse.bacc as bacc
    from concourse.bass_utils import run_bass_kernel_spmd

    x, src, dst, edge = (np.asarray(a) for a in (x, src, dst, edge_attr_32))
    pad = EDGES - N_EDGES
    src_p = np.concatenate([src, np.zeros(pad, src.dtype)])
    dst_p = np.concatenate([dst, np.full(pad, N_NODES, dst.dtype)])
    edge_p = np.concatenate([edge, np.zeros((pad, DE), edge.dtype)])
    x_p = np.concatenate([x, np.zeros((NODES - N_NODES, D), x.dtype)])
    src_tiles = np.ascontiguousarray(src_p.reshape(TILES, P).T)
    arrays = {
        "x_rows": x,
        "x_t": np.ascontiguousarray(x_p.T),
        "src_first": np.ascontiguousarray(src_tiles[:, :UNROLL * TPG]),
        "src_all": src_tiles,
        "dst_groups": dst_p.reshape(GROWS, GPP * GE),
        "dst_tiles": np.ascontiguousarray(dst_p.reshape(TILES, P).T),
        "edge_t": np.ascontiguousarray(edge_p.T),
        "mw1": np.asarray(L0_gnn_mW1), "mb1": np.asarray(L0_gnn_mb1),
        "mw2": np.asarray(L0_gnn_mW2), "mb2": np.asarray(L0_gnn_mb2),
        "uw1": np.asarray(L0_gnn_uW1), "ub1": np.asarray(L0_gnn_ub1),
        "uw2": np.asarray(L0_gnn_uW2), "ub2": np.asarray(L0_gnn_ub2),
    }
    nc = bacc.Bacc("TRN2", target_bir_lowering=False, num_devices=1)
    args = [nc.dram_tensor(name, a.shape, mybir.dt.from_np(a.dtype), kind="ExternalInput").ap()
            for name, a in arrays.items()]
    out = nc.dram_tensor("out", (N_NODES, D), mybir.dt.float32, kind="ExternalOutput").ap()
    build(nc, *args, out)
    return run_bass_kernel_spmd(nc, [arrays], core_ids=[0]).results[0]["out"]
```

```python
import concourse.bass as bass
from concourse import mybir
from contextlib import ExitStack

N_NODES = 12500
N_EDGES = 200000
D = 64
DE = 32
DH = 128
P = 128

TPG = 4
GE = TPG * P
UNROLL = 8
GROUPS = -(-N_EDGES // (GE * UNROLL)) * UNROLL
ITERS = GROUPS // UNROLL
EDGES = GROUPS * GE
TILES = GROUPS * TPG
GPP = 4
GROWS = GROUPS // GPP
G_END = -(-N_EDGES // GE)
T_END = -(-N_EDGES // P)
WIN = 96
CB = 4
CHUNKS = -(-N_NODES // (P * CB))
CN = CB * P
CW = CB * D
BLOCKS = CHUNKS * CB
NODES = BLOCKS * P
REAL_BLOCKS = N_NODES // P
LAST_BASE = NODES - WIN
RING = 4
KX = D + DE + 1
TRASH = NODES
AGG_ROWS = NODES + P
AGG_W = DH + 1
TAIL = 2
UPD_LAP = ITERS - CHUNKS + TAIL
TB = 4
TSTEPS = -(-BLOCKS // TB)
TSLOTS = 5
EPS = 1e-5
assert EDGES == TILES * P and GROWS * GPP == GROUPS and CHUNKS % TAIL == 1
assert (ITERS - 1) * UNROLL < G_END <= GROUPS and 2 * GPP == UNROLL and TSTEPS % TSLOTS == 0


def build(nc, x_rows, x_t, src_first, src_all, dst_groups, dst_tiles, edge_t,
          mw1, mb1, mw2, mb2, uw1, ub1, uw2, ub2, out):
    f32 = mybir.dt.float32
    i32 = mybir.dt.int32
    bf16 = mybir.dt.bfloat16
    ALU = mybir.AluOpType
    ACT = mybir.ActivationFunctionType
    X = mybir.AxisListType.X
    ds = bass.ds
    ET = mybir.EngineType

    ctx = ExitStack()
    with ctx:
        def sb(name, shape, dt=f32):
            return ctx.enter_context(nc.sbuf_tensor(name, shape, dt))

        def sem(name):
            return ctx.enter_context(nc.semaphore(name))

        def dram(name, shape, dt=f32):
            return nc.dram_tensor(name, shape, dt, kind="Internal").ap()

        table = dram("dst_table", (NODES, DH))
        base_i_dram = dram("window_base_i", (GROUPS,), i32)
        base_f_dram = dram("window_base_f", (GROUPS,))
        spread_dram = dram("window_spread", (GROUPS,))
        lag_dram = dram("window_lag", (GROUPS,))
        agg_dram = dram("agg_rows", (AGG_ROWS, AGG_W))

        ident = sb("ident", [P, P])
        ident_bf = sb("ident_bf", [P, P], bf16)
        eps = sb("eps", [P, 1])
        iota_i = sb("iota_i", [P, WIN], i32)
        iota = sb("iota", [P, WIN])
        ones_bf = sb("ones_bf", [P, P], bf16)
        w_xe = sb("w_xe", [KX, DH])
        w_dst = sb("w_dst", [D, DH])
        w2_pad = sb("w2_pad", [DH, P])
        b2_col = sb("b2_col", [P, 1])
        u1 = sb("u1", [2 * D, DH])
        c1_col = sb("c1_col", [DH, 1])
        u2 = sb("u2", [DH, D])
        c2_rows = sb("c2_rows", [P, D])

        agg_t = sb("agg_t", [DH, NODES])
        xc = sb("xc", [P, NODES])
        resid = sb("resid", [P, BLOCKS * D])

        src_idx = sb("src_idx", [P, TILES + TPG], i32)
        slot_idx = sb("slot_idx", [P, UNROLL * TPG], i32)
        dst_i = sb("dst_i", [P, TILES], i32)
        rel = sb("rel", [P, TILES])
        base_row = sb("base_row", [1, GROUPS], i32)
        spread_row = sb("spread_row", [1, GROUPS])
        lag_row = sb("lag_row", [1, GROUPS])
        path = sb("path", [1, 2], i32)
        lag_i = sb("lag_i", [GROWS, 1], i32)
        lag_f = sb("lag_f", [GROWS, 1])
        lag = sb("lag", [GROWS, GPP])
        base_mn = sb("base_mn", [GROWS, GPP])
        base_f = sb("base_f", [GROWS, GPP])
        base_i = sb("base_i", [GROWS, GPP], i32)
        dst_mx = sb("dst_mx", [GROWS, GPP])
        spread = sb("spread", [GROWS, GPP])

        xg = sb("xg", [P, UNROLL, TPG * D])
        xe = sb("xe", [KX, RING, GE])
        x_win = sb("x_win", [D, 2, WIN])
        win_tab = sb("win_tab", [WIN, RING, DH])
        oh = sb("oh", [P, RING, TPG * WIN])
        oh_t = sb("oh_t", [WIN, 2, GE])
        hid = sb("hid", [P, 2, TPG * DH])

        dst_g = resid[0:GROWS, 0:GPP * GE].bitcast(i32)
        dst_g_real = resid[0:GROWS, GPP * GE:2 * GPP * GE]
        base_all = resid[:, 2 * GPP * GE:2 * GPP * GE + GROUPS]
        tab_out = [hid[:, 0, :], hid[:, 1, :]] + [rel[:, n * TB * DH:(n + 1) * TB * DH]
                                                  for n in range(TSLOTS - 2)]
        upd_h = [dst_i[:, v * CN:(v + 1) * CN].bitcast(f32) for v in range(TAIL)]
        upd_sq = [dst_i[:, TAIL * CN + v * CW:][:, 0:CW].bitcast(f32) for v in range(TAIL)]

        banks = [ctx.enter_context(nc.psum_tensor(f"bank{i}", [P, 512], f32)) for i in range(8)]
        ps_x, ps_h, ps_a, ps_o = banks[0:2], banks[2:4], banks[4:6], banks[6]

        s_first = sem("s_first")
        s_src = sem("s_src")
        s_dstg = sem("s_dstg")
        s_dstt = sem("s_dstt")
        s_wmsg = sem("s_wmsg")
        s_wdst = sem("s_wdst")
        s_wupd = sem("s_wupd")
        s_resid = sem("s_resid")
        s_xt = sem("s_xt")
        s_const = sem("s_const")
        s_iota = sem("s_iota")
        s_ident = sem("s_ident")
        s_iotaf = sem("s_iotaf")
        s_ident_bf = sem("s_ident_bf")
        s_zero_dve = sem("s_zero_dve")
        s_zero_act = sem("s_zero_act")
        s_zero_w2 = sem("s_zero_w2")
        s_one_row = sem("s_one_row")
        s_win = sem("s_win")
        s_base = sem("s_base")
        s_scratch = sem("s_scratch")
        s_back = sem("s_back")
        s_flag = sem("s_flag")
        s_rel = sem("s_rel")
        s_lag = sem("s_lag")
        s_tab_mm = sem("s_tab_mm")
        s_tab_cp = sem("s_tab_cp")
        s_tab_st = [sem(f"s_tab_st{n}") for n in range(TSLOTS)]
        s_gathered = [sem(f"s_gathered{i}") for i in range(UNROLL)]
        s_edge = [sem(f"s_edge{i}") for i in range(RING)]
        s_idx = sem("s_idx")
        s_opened = sem("s_opened")
        s_picked = sem("s_picked")
        s_xt_mm = sem("s_xt_mm")
        s_xe = sem("s_xe")
        s_oh = sem("s_oh")
        s_oht_mm = sem("s_oht_mm")
        s_oht = sem("s_oht")
        s_h = sem("s_h")
        s_relu = sem("s_relu")
        s_agg = sem("s_agg")
        s_added = sem("s_added")
        s_c2 = sem("s_c2")
        s_m1 = sem("s_m1")
        s_u = sem("s_u")
        s_m2 = sem("s_m2")
        s_hu = sem("s_hu")
        s_m3 = sem("s_m3")
        s_sum = sem("s_sum")
        s_summed = sem("s_summed")
        s_mean = sem("s_mean")
        s_red = sem("s_red")
        s_dev = sem("s_dev")
        s_sq = sem("s_sq")
        s_var = sem("s_var")
        s_std = sem("s_std")
        s_rstd = sem("s_rstd")
        s_norm = sem("s_norm")
        s_out = sem("s_out")

        def wait(eng, s, n):
            if not isinstance(n, int) or n > 0:
                eng.wait_ge(s, n)

        def upper_halves(ap):
            return ap.bitcast(bf16).rearrange("p (n two) -> p n two", two=2)[:, :, 1]

        def gather(pool, g, k, tiles=TPG):
            wait(pool, s_idx, g - UNROLL + 1)
            pool.sem_inc(s_opened, 1)
            for j in range(tiles):
                c = k * TPG + j
                pool.indirect_dma_start(
                    out=xg[:, k, j * D:(j + 1) * D], out_offset=None, in_=x_rows,
                    in_offset=bass.IndirectOffsetOnAxis(ap=slot_idx[:, c:c + 1], axis=0),
                ).then_inc(s_gathered[k], 16)

        def load_edges(sp, g, k):
            r = k % RING
            wait(sp, s_h, g - RING + 1)
            sp.dma_start(xe[D:D + DE, r, :], edge_t[:, ds(g * GE, GE)]).then_inc(s_edge[r], 16)

        def transpose_x(pe, g, k, lap):
            q = k % 2
            missing = G_END * TPG - T_END if isinstance(g, int) and g == G_END - 1 else 0
            wait(pe, s_gathered[k], (lap + 1) * 16 * TPG - 16 * missing)
            wait(pe, s_xe, g - 1)
            for m in range(TPG // 2):
                nc.tensor.transpose(ps_x[q][:, m * P:(m + 1) * P],
                                    xg[:, k, m * 2 * D:(m + 1) * 2 * D], ident[:, :])
            wait(pe, s_picked, g + 1)
            nc.tensor.matmul(ps_x[q][0:WIN, GE // 2:GE // 2 + DH], x_win[:, q, :], w_dst[:, :],
                             start=True, stop=True).then_inc(s_xt_mm, 1)

        def transpose_oh(pe, g, k):
            r = k % RING
            wait(pe, s_oh, g + 1)
            wait(pe, s_oht, g)
            half = upper_halves(oh[:, r, :])
            for j in range(TPG):
                last = nc.tensor.matmul(ps_o[0:WIN, j * P:(j + 1) * P], half[:, j * WIN:(j + 1) * WIN],
                                        ident_bf[:, :], start=True, stop=True)
            last.then_inc(s_oht_mm, 1)

        def hidden(pe, g, k, lap):
            q, r = k % 2, k % RING
            n = lap * (UNROLL // RING) + k // RING + 1
            wait(pe, s_xe, g + 1)
            wait(pe, s_edge[r], n * 16)
            wait(pe, s_oht, g + 1)
            wait(pe, s_relu, g - 1)
            for j in range(TPG):
                o = ps_h[q][:, j * DH:(j + 1) * DH]
                nc.tensor.matmul(o, xe[:, r, j * P:(j + 1) * P], w_xe[:, :], start=True, stop=False)
                last = nc.tensor.matmul(o, oh_t[:, q, j * P:(j + 1) * P], win_tab[:, r, :],
                                        start=False, stop=True)
            last.then_inc(s_h, 1)

        def aggregate(pe, g, k):
            q, r = k % 2, k % RING
            wait(pe, s_relu, g + 1)
            wait(pe, s_added, g - 1)
            for j in range(TPG):
                nc.tensor.matmul(ps_a[q][:, 0:WIN], hid[:, q, j * DH:(j + 1) * DH],
                                 oh[:, r, j * WIN:(j + 1) * WIN], start=(j == 0), stop=(j == TPG - 1))
            half = upper_halves(oh[:, r, :])
            for j in range(TPG):
                last = nc.tensor.matmul(ps_a[q][:, WIN:2 * WIN], ones_bf[:, :],
                                        half[:, j * WIN:(j + 1) * WIN],
                                        start=(j == 0), stop=(j == TPG - 1))
            last.then_inc(s_agg, 1)

        def copy_x(g, k):
            act = nc.scalar
            q, r = k % 2, k % RING
            wait(act, s_xt_mm, g + 1)
            wait(act, s_h, g - RING + 1)
            to = xe[0:D, r, :].rearrange("p (m t e) -> p m t e", t=2, e=P)
            for t in range(2):
                of = ps_x[q][t * D:(t + 1) * D, 0:GE // 2].rearrange("p (m e) -> p m e", e=P)
                act.activation(to[:, :, t, :], of, ACT.Copy)
            act.activation(win_tab[:, r, :], ps_x[q][0:WIN, GE // 2:GE // 2 + DH], ACT.Copy
                           ).then_inc(s_xe, 1)

        def pick_window(g, k, base):
            q = k % 2
            wait(nc.scalar, s_xt_mm, g - 1)
            nc.scalar.activation(x_win[:, q, :], xc[0:D, ds(base, WIN)], ACT.Copy).then_inc(s_picked, 1)

        def relu(g, k):
            act = nc.scalar
            q = k % 2
            wait(act, s_h, g + 1)
            wait(act, s_agg, g - 1)
            act.activation(hid[:, q, :], ps_h[q][:, :], ACT.Relu).then_inc(s_relu, 1)

        def one_hot(g, k):
            dve = nc.vector
            r = k % RING
            wait(dve, s_agg, g - RING + 1)
            grid = [P, TPG, WIN]
            dve.tensor_tensor(oh[:, r, :].rearrange("p (j w) -> p j w", w=WIN),
                              iota[:, None, :].to_broadcast(grid),
                              rel[:, ds(g * TPG, TPG)][:, :, None].to_broadcast(grid),
                              ALU.is_equal).then_inc(s_oh, 1)

        def copy_oh(g, k):
            dve = nc.vector
            q = k % 2
            wait(dve, s_oht_mm, g + 1)
            wait(dve, s_h, g - 1)
            dve.tensor_copy(oh_t[:, q, :], ps_o[0:WIN, :]).then_inc(s_oht, 1)

        def next_indices(g, k):
            dve = nc.vector
            wait(dve, s_xt_mm, g + 1)
            dve.tensor_copy(slot_idx[:, k * TPG:(k + 1) * TPG],
                            src_idx[:, ds((g + UNROLL) * TPG, TPG)]).then_inc(s_idx, 1)

        def add_window(g, k, base):
            dve = nc.vector
            q = k % 2
            wait(dve, s_agg, g + 1)
            wait(dve, s_added, g)
            to, cnt = agg_t[:, ds(base, WIN)], xc[D:P, ds(base, WIN)]
            dve.tensor_tensor(to, ps_a[q][:, 0:WIN], to, ALU.add)
            dve.tensor_tensor(cnt, ps_a[q][D:P, WIN:2 * WIN], cnt, ALU.add).then_inc(s_added, 1)

        def window_bases(eng, start, n):
            return nc.values_load_multi_w_load_instructions(
                base_row[0:1, ds(start, n)], engines=(eng,), min_val=0, max_val=LAST_BASE,
                skip_runtime_bounds_check_because="the chip clamps them to this range")[1]

        def table_stored(eng):
            for n in range(TSLOTS):
                eng.wait_ge(s_tab_st[n], TSTEPS // TSLOTS * 16)

        def laps(eng, lap, open_update, chunk):
            lap(0, None)
            with eng.Fori(1, UPD_LAP) as i:
                lap(i, None)
            open_update()
            behind = eng.value_load(path[0:1, 1:2], min_val=0, max_val=NODES)
            with eng.If(behind < 1):
                with eng.Fori(UPD_LAP, ITERS - 1) as i:
                    lap(i, i - UPD_LAP)
                lap(ITERS - 1, CHUNKS - TAIL - 1)
                chunk([CHUNKS - 2, CHUNKS - 1])
            with eng.Else():
                with eng.Fori(UPD_LAP, ITERS - 1) as i:
                    lap(i, None)
                lap(ITERS - 1, None)
                all_chunks(eng, chunk)

        def all_chunks(eng, chunk):
            with eng.Fori(0, CHUNKS // TAIL) as n:
                chunk([n * TAIL + v for v in range(TAIL)])
            chunk([CHUNKS - 1])

        def exists(g):
            return not isinstance(g, int) or g < G_END

        def windows_fit(eng, body, other):
            eng.wait_ge(s_flag, 2)
            widest = eng.value_load(path[0:1, 0:1], min_val=0, max_val=NODES)
            with eng.If(widest < WIN):
                body()
            with eng.Else():
                other()

        g_x = xg[:, 0, 0:P]
        g_tab = hid[:, 0, 0:DH]
        g_dcol = rel[:, 0:1]
        g_dbc = hid[:, 0, DH:2 * DH]
        g_same = hid[:, 0, 2 * DH:3 * DH]
        g_low = hid[:, 0, 3 * DH:4 * DH]
        g_pre = hid[:, 1, 0:DH]
        g_h = oh[:, 0, 0:AGG_W]
        g_sum = oh[:, 1, 0:AGG_W]
        g_earlier = hid[:, 1, 2 * DH:3 * DH]
        g_scr = rel[:, 8:16]
        g_xe = xe[:, 0, 0:P]
        g_back = oh[:, 2, 0:AGG_W]
        g_cbc = hid[:, 1, 3 * DH:4 * DH]
        g_si, g_di, g_to = slot_idx[:, 0:1], slot_idx[:, 1:2], slot_idx[:, 2:3]
        t_zero = sem("t_zero")
        t_init = sem("t_init")
        t_low = sem("t_low")
        t_gat = sem("t_gat")
        t_edge = sem("t_edge")
        t_tr = sem("t_tr")
        t_xe = sem("t_xe")
        t_h = sem("t_h")
        t_same = sem("t_same")
        t_pre = sem("t_pre")
        t_relu = sem("t_relu")
        t_sum = sem("t_sum")
        t_step = sem("t_step")
        t_out = sem("t_out")
        t_scat = sem("t_scat")
        t_rows = sem("t_rows")
        t_cbc = sem("t_cbc")
        t_btr = sem("t_btr")
        t_bcp = sem("t_bcp")
        DVE_STEPS = 4

        def general_pool():
            pool = nc.gpsimd
            for k in range(UNROLL):
                pool.wait_ge(s_gathered[k], 16 * TPG)
            table_stored(pool)
            pool.memset(g_x[:, D:P], 0.0).then_inc(t_zero, 1)
            pool.memset(g_low, 1.0).then_inc(t_low, 1)
            pool.wait_ge(t_low, 1)
            pool.affine_select(out=g_low, in_=g_low, compare_op=ALU.is_gt, fill=0.0, base=0,
                               pattern=[[-1, P]], channel_multiplier=1).then_inc(t_low, 1)
            with pool.Fori(0, T_END) as t:
                pool.wait_ge(t_step, t * DVE_STEPS + 1)
                pool.sem_inc(s_opened, 1)
                pool.indirect_dma_start(
                    out=g_x[:, 0:D], out_offset=None, in_=x_rows,
                    in_offset=bass.IndirectOffsetOnAxis(ap=g_si, axis=0)).then_inc(t_gat, 16)
                pool.indirect_dma_start(
                    out=g_tab, out_offset=None, in_=table,
                    in_offset=bass.IndirectOffsetOnAxis(ap=g_di, axis=0)).then_inc(t_gat, 16)
                pool.wait_ge(t_out, t + 1)
                pool.sem_inc(s_opened, 1)
                pool.indirect_dma_start(
                    out=agg_dram, out_offset=bass.IndirectOffsetOnAxis(ap=g_to, axis=0),
                    in_=g_sum, in_offset=None, compute_op=ALU.add).then_inc(t_scat, 16)

        def general_sync():
            sp = nc.sync
            half = AGG_ROWS * AGG_W // P // 2
            rows = agg_dram.rearrange("(p r) w -> p (r w)", p=P)
            sp.wait_ge(s_zero_act, 1)
            at = 0
            for n in (half, rows.shape[1] - half):
                sp.dma_start(rows[:, at:at + n], agg_t[:, 0:n]).then_inc(t_init, 16)
                at += n
            with sp.Fori(0, T_END) as t:
                sp.wait_ge(t_step, t * DVE_STEPS + 1)
                sp.dma_start(g_xe[D:D + DE, :], edge_t[:, ds(t * P, P)]).then_inc(t_edge, 16)
            sp.wait_ge(t_scat, T_END * 16)
            with sp.Fori(0, BLOCKS) as b:
                sp.wait_ge(t_bcp, b + 1)
                sp.dma_start(g_back, agg_dram[ds(b * P, P), :]).then_inc(t_rows, 16)

        def general_tensor():
            pe = nc.tensor
            for n in range(TSTEPS):
                wait(pe, s_tab_cp, n - 3)
                for b in range(min(TB, BLOCKS - n * TB)):
                    at = (n * TB + b) * P
                    last = nc.tensor.matmul(banks[n % 4][:, b * DH:(b + 1) * DH], xc[0:D, at:at + P],
                                            w_dst[:, :], start=True, stop=True)
                last.then_inc(s_tab_mm, 1)
            pe.wait_ge(s_tab_cp, TSTEPS)
            pe.wait_ge(t_zero, 1)
            with pe.Fori(0, T_END) as t:
                pe.wait_ge(t_gat, (t + 1) * 32)
                pe.wait_ge(t_step, t * DVE_STEPS + 2)
                nc.tensor.transpose(ps_x[0][:, 0:P], g_x, ident[:, :])
                nc.tensor.transpose(ps_o[:, 0:P], g_dbc, ident[:, :]).then_inc(t_tr, 1)
                pe.wait_ge(t_xe, t + 1)
                pe.wait_ge(t_edge, (t + 1) * 16)
                nc.tensor.matmul(ps_h[0][:, 0:DH], g_xe, w_xe[:, :],
                                 start=True, stop=True).then_inc(t_h, 1)
                pe.wait_ge(t_same, t + 1)
                pe.wait_ge(t_relu, t + 1)
                nc.tensor.matmul(ps_a[0][:, 0:AGG_W], g_same, g_h,
                                 start=True, stop=True).then_inc(t_sum, 1)
            with pe.Fori(0, BLOCKS) as b:
                pe.wait_ge(t_cbc, b + 1)
                nc.tensor.transpose(ps_x[0][:, 0:P], g_back[:, 0:DH], ident[:, :])
                nc.tensor.transpose(ps_o[:, 0:P], g_cbc, ident[:, :]).then_inc(t_btr, 1)

        def general_scalar():
            act = nc.scalar
            act.wait_ge(s_rel, 1)
            for n in range(TSTEPS + 1):
                if n < TSTEPS:
                    w = min(TB, BLOCKS - n * TB) * DH
                    act.wait_ge(s_tab_mm, n + 1)
                    if n >= TSLOTS:
                        act.wait_ge(s_tab_st[n % TSLOTS], n // TSLOTS * 16)
                    act.activation(tab_out[n % TSLOTS][:, 0:w], banks[n % 4][:, 0:w],
                                   ACT.Copy).then_inc(s_tab_cp, 1)
                if n > 0:
                    act.wait_ge(s_tab_cp, n)
                    nb = min(TB, BLOCKS - (n - 1) * TB)
                    act.dma_start(table[(n - 1) * TB * P:((n - 1) * TB + nb) * P, :].rearrange(
                                      "(b p) n -> p b n", p=P),
                                  tab_out[(n - 1) % TSLOTS][:, 0:nb * DH].rearrange(
                                      "p (b n) -> p b n", n=DH)).then_inc(s_tab_st[(n - 1) % TSLOTS], 16)
            with act.Fori(0, T_END) as t:
                act.wait_ge(t_tr, t + 1)
                act.activation(g_xe[0:D, :], ps_x[0][0:D, 0:P], ACT.Copy).then_inc(t_xe, 1)
                act.wait_ge(t_pre, t + 1)
                act.activation(g_h[:, 0:DH], g_pre, ACT.Relu).then_inc(t_relu, 1)

        def general_vector():
            dve = nc.vector
            table_stored(dve)
            dve.wait_ge(s_src, 16)
            dve.wait_ge(t_low, 2)
            dve.wait_ge(t_init, 32)
            dve.memset(g_h[:, DH:AGG_W], 1.0).then_inc(t_bcp, 1)
            dve.wait_ge(t_bcp, 1)
            with dve.Fori(0, T_END) as t:
                at = t * DVE_STEPS
                dve.tensor_copy(g_si, src_idx[:, ds(t, 1)])
                dve.tensor_copy(g_dcol, dst_i[:, ds(t, 1)])
                dve.tensor_copy(g_di, dst_i[:, ds(t, 1)]).then_inc(t_step, 1)
                dve.wait_ge(t_step, at + 1)
                dve.tensor_copy(g_dbc, g_dcol.to_broadcast([P, P])).then_inc(t_step, 1)
                dve.wait_ge(t_tr, t + 1)
                dve.tensor_scalar(g_same, ps_o[:, 0:P], g_dcol, None, ALU.is_equal).then_inc(t_same, 1)
                dve.wait_ge(t_h, t + 1)
                dve.tensor_tensor(g_pre, ps_h[0][:, 0:DH], g_tab, ALU.add).then_inc(t_pre, 1)
                dve.wait_ge(t_same, t + 1)
                dve.tensor_tensor(g_earlier, g_same, g_low, ALU.mult).then_inc(t_step, 1)
                dve.wait_ge(t_step, at + 3)
                dve.reduce_max(g_scr[:, 0:1], g_earlier, X).then_inc(t_step, 1)
                dve.wait_ge(t_step, at + 4)
                general_row(dve, t)
                dve.wait_ge(t_sum, t + 1)
                dve.tensor_copy(g_sum, ps_a[0][:, 0:AGG_W]).then_inc(t_out, 1)
                dve.wait_ge(t_scat, (t + 1) * 16)

            with dve.Fori(0, BLOCKS) as b:
                dve.wait_ge(t_rows, (b + 1) * 16)
                dve.tensor_copy(g_cbc, g_back[:, DH:AGG_W].to_broadcast([P, P])).then_inc(t_cbc, 1)
                dve.wait_ge(t_btr, b + 1)
                dve.tensor_copy(agg_t[:, ds(b * P, P)], ps_x[0][:, 0:P])
                dve.tensor_copy(xc[D:P, ds(b * P, P)], ps_o[D:P, 0:P]).then_inc(t_bcp, 1)
            dve.wait_ge(t_bcp, BLOCKS + 1)

        t_row = sem("t_row")
        trash_f = sb("trash_f", [P, 1])
        trash_i = sb("trash_i", [P, 1], i32)

        def general_row(dve, t):
            dve.tensor_tensor(g_scr[:, 1:2], trash_f[:, :], g_dcol, ALU.subtract).then_inc(t_row, 1)
            dve.wait_ge(t_row, t * 2 + 1)
            dve.tensor_tensor(g_scr[:, 2:3], g_scr[:, 1:2], g_scr[:, 0:1], ALU.mult).then_inc(t_row, 1)
            dve.wait_ge(t_row, t * 2 + 2)
            dve.tensor_tensor(g_to, g_scr[:, 2:3], g_dcol, ALU.add)

        stat = sb("stat", [P, TAIL, 4 * CB])

        def stats(c, v):
            return [stat[:, v or 0, n * CB:n * CB + filled(c)] for n in range(4)]

        def filled(c):
            return REAL_BLOCKS + 1 - c * CB if isinstance(c, int) and c == CHUNKS - 1 else CB

        def bank_of(v, n):
            return banks[7] if v is None else banks[v * 3 + n]

        def columns_of(t, c):
            return t[:, ds(c * CN, filled(c) * P)]

        def rows_of(c):
            return resid[:, ds(c * CW, filled(c) * D)]

        def blocks(ap):
            return ap.rearrange("p (b d) -> p b d", d=D)

        def pe_m1(c, v=None):
            pe = nc.tensor
            pe.wait_ge(s_c2, c + 1)
            nc.tensor.matmul(bank_of(v, 0)[:, 0:filled(c) * P], w2_pad[:, :], columns_of(agg_t, c),
                             start=True, stop=True).then_inc(s_m1, 1)

        def pe_m2(c, v=None):
            pe = nc.tensor
            pe.wait_ge(s_u, c + 1)
            nc.tensor.matmul(bank_of(v, 1)[:, 0:filled(c) * P], u1[:, :], columns_of(xc, c),
                             start=True, stop=True).then_inc(s_m2, 1)

        def pe_m3(c, v=None):
            pe = nc.tensor
            pe.wait_ge(s_hu, c + 1)
            for b in range(filled(c)):
                last = nc.tensor.matmul(bank_of(v, 2)[:, b * D:(b + 1) * D],
                                        upd_h[v or 0][:, b * P:(b + 1) * P], u2[:, :],
                                        start=True, stop=True)
            last.then_inc(s_m3, 1)

        def dve_c2(c):
            y = blocks(rows_of(c))
            nc.vector.tensor_tensor(y, y, c2_rows[:, None, :].to_broadcast([P, filled(c), D]), ALU.add
                                    ).then_inc(s_c2, 1)

        def dve_stack(c, v=None):
            dve = nc.vector
            dve.wait_ge(s_m1, c + 1)
            cnt = columns_of(xc, c)[D:P, :]
            dve.scalar_tensor_tensor(cnt, cnt, b2_col[D:P, 0:1], bank_of(v, 0)[D:P, 0:filled(c) * P],
                                     ALU.mult, ALU.add).then_inc(s_u, 1)

        def act_relu(c, v=None):
            act = nc.scalar
            act.wait_ge(s_m2, c + 1)
            n = filled(c) * P
            act.activation(upd_h[v or 0][:, 0:n], bank_of(v, 1)[:, 0:n], ACT.Relu, bias=c1_col[:, 0:1]
                           ).then_inc(s_hu, 1)

        def dve_center(c, v=None):
            dve = nc.vector
            y = rows_of(c)
            total, mean, _, _ = stats(c, v)
            dve.wait_ge(s_m3, c + 1)
            dve.tensor_tensor(y, bank_of(v, 2)[:, 0:filled(c) * D], y, ALU.add).then_inc(s_sum, 1)
            dve.wait_ge(s_sum, c + 1)
            dve.sem_inc(s_summed, 1)
            dve.reduce_sum(total, blocks(y), X).then_inc(s_red, 1)
            dve.wait_ge(s_red, c + 1)
            dve.tensor_scalar(mean, total, 1.0 / D, None, ALU.mult).then_inc(s_mean, 1)
            dve.wait_ge(s_mean, c + 1)
            dve.tensor_tensor(blocks(y), blocks(y), mean[:, :, None].to_broadcast([P, filled(c), D]),
                              ALU.subtract).then_inc(s_dev, 1)

        def act_square(c, v=None):
            act = nc.scalar
            act.wait_ge(s_dev, c + 1)
            act.activation(upd_sq[v or 0][:, 0:filled(c) * D], rows_of(c), ACT.Square).then_inc(s_sq, 1)

        def dve_variance(c, v=None):
            dve = nc.vector
            dve.wait_ge(s_sq, c + 1)
            dve.reduce_sum(stats(c, v)[2], blocks(upd_sq[v or 0][:, 0:filled(c) * D]), X).then_inc(s_var, 1)

        def act_deviation(c, v=None):
            act = nc.scalar
            act.wait_ge(s_var, c + 1)
            act.activation(stats(c, v)[3], stats(c, v)[2], ACT.Sqrt, bias=eps[:, 0:1], scale=1.0 / D
                           ).then_inc(s_std, 1)

        def dve_normalize(c, v=None):
            dve = nc.vector
            y = blocks(rows_of(c))
            rstd, _, _, std = stats(c, v)
            dve.wait_ge(s_std, c + 1)
            dve.reciprocal(rstd, std).then_inc(s_rstd, 1)
            dve.wait_ge(s_rstd, c + 1)
            dve.tensor_tensor(y, y, rstd[:, :, None].to_broadcast([P, filled(c), D]), ALU.mult
                              ).then_inc(s_norm, 1)

        def act_store(c):
            act = nc.scalar
            act.wait_ge(s_norm, c + 1)
            if isinstance(c, int) and c == CHUNKS - 1:
                whole, rest = divmod(N_NODES - c * CN, P)
                act.dma_start(out[c * CN + whole * P:, :],
                              rows_of(c)[0:rest, whole * D:(whole + 1) * D]).then_inc(s_out, 16)
            else:
                whole = CB
            act.dma_start(out[ds(c * CN, whole * P), :].rearrange("(b p) d -> p b d", p=P),
                          blocks(rows_of(c))[:, 0:whole, :]).then_inc(s_out, 16)

        def each(stage, cs):
            for v, c in enumerate(cs):
                stage(c, v)

        def pe_chunks(cs):
            each(pe_m1, cs)
            each(pe_m2, cs)
            each(pe_m3, cs)

        def act_chunks(cs):
            each(act_relu, cs)
            each(act_square, cs)
            each(act_deviation, cs)
            for c in cs:
                act_store(c)

        def dve_chunks(cs):
            for c in cs:
                dve_c2(c)
            each(dve_stack, cs)
            each(dve_center, cs)
            each(dve_variance, cs)
            each(dve_normalize, cs)

        block = ctx.enter_context(nc.Block())

        @block.gpsimd
        def _(pool):
            pool.iota(iota_i[:, :], pattern=[[1, WIN]], base=0, channel_multiplier=0).then_inc(s_iota, 1)
            pool.memset(ident[:, :], 0.0).then_inc(s_ident, 1)
            pool.wait_ge(s_ident, 1)
            pool.affine_select(out=ident[:, :], in_=ident[:, :], compare_op=ALU.not_equal, fill=1.0,
                               base=0, pattern=[[-1, P]], channel_multiplier=1).then_inc(s_ident, 1)
            pool.iota(trash_i[:, :], pattern=[[0, 1]], base=TRASH, channel_multiplier=1).then_inc(s_iota, 1)
            pool.iota(lag_i[:, :], pattern=[[0, 1]], base=(1 - UPD_LAP) * CN, channel_multiplier=CN // 2
                      ).then_inc(s_iota, 1)
            pool.wait_ge(s_first, 16)
            for k in range(UNROLL):
                gather(pool, k, k)

            def windowed():
                with pool.Fori(1, ITERS - 1) as i:
                    for k in range(UNROLL):
                        gather(pool, i * UNROLL + k, k)
                for g in range((ITERS - 1) * UNROLL, G_END):
                    gather(pool, g, g % UNROLL, min(TPG, T_END - g * TPG))

            windows_fit(pool, windowed, general_pool)

        @block.sync
        def _(sp):
            sp.dma_start(slot_idx[:, :], src_first).then_inc(s_first, 16)
            sp.dma_start(dst_g, dst_groups).then_inc(s_dstg, 16)
            sp.dma_start(w_xe[0:D, :], mw1[0:D, :]).then_inc(s_wmsg, 16)
            sp.dma_start(w_xe[D:D + DE, :], mw1[2 * D:2 * D + DE, :]).then_inc(s_wmsg, 16)
            sp.dma_start(w_xe[D + DE:KX, :], mb1[None, :]).then_inc(s_wmsg, 16)
            sp.wait_ge(s_win, 5)
            for to, of in ((base_f_dram, base_f), (spread_dram, spread), (lag_dram, lag), (base_i_dram, base_i)):
                sp.dma_start(to.rearrange("(p g) -> p g", g=GPP), of[:, :]).then_inc(s_scratch, 16)
            sp.wait_ge(s_scratch, 64)
            sp.dma_start(base_all, base_f_dram[None, :].to_broadcast([P, GROUPS])).then_inc(s_back, 16)
            sp.dma_start(spread_row[:, :], spread_dram[None, :]).then_inc(s_back, 16)
            sp.dma_start(lag_row[:, :], lag_dram[None, :]).then_inc(s_back, 16)
            sp.dma_start(base_row[:, :], base_i_dram[None, :]).then_inc(s_back, 16)
            sp.dma_start(src_idx[:, 0:TILES], src_all).then_inc(s_src, 16)

            def load_weights():
                sp.wait_ge(s_zero_w2, 2)
                sp.dma_start(w2_pad[:, D:P], mw2).then_inc(s_wupd, 16)
                sp.dma_start(b2_col[D:P, :], mb2[:, None]).then_inc(s_wupd, 16)
                sp.dma_start(u1[:, :], uw1).then_inc(s_wupd, 16)
                sp.dma_start(c1_col[:, :], ub1[:, None]).then_inc(s_wupd, 16)
                sp.dma_start(u2[:, :], uw2).then_inc(s_wupd, 16)
                sp.dma_start(c2_rows[:, :], ub2[None, :].to_broadcast([P, D])).then_inc(s_wupd, 16)

            def load_x(c):
                if isinstance(c, int) and c == CHUNKS - 1:
                    whole, rest = divmod(N_NODES - c * CN, P)
                    sp.dma_start(resid[0:rest, (c * CB + whole) * D:(c * CB + whole + 1) * D],
                                 x_rows[c * CN + whole * P:, :]).then_inc(s_resid, 16)
                else:
                    whole = CB
                sp.dma_start(blocks(rows_of(c))[:, 0:whole, :],
                             x_rows[ds(c * CN, whole * P), :].rearrange("(b p) d -> p b d", p=P)
                             ).then_inc(s_resid, 16)

            def windowed():
                def lap(i):
                    for k in range(UNROLL):
                        if exists(i * UNROLL + k):
                            load_edges(sp, i * UNROLL + k, k)
                lap(0)
                load_weights()
                with sp.Fori(1, CHUNKS) as i:
                    load_x(i - 1)
                    lap(i)
                load_x(CHUNKS - 1)
                with sp.Fori(CHUNKS, ITERS - 1) as i:
                    lap(i)
                lap(ITERS - 1)

            def general():
                load_weights()
                with sp.Fori(0, CHUNKS - 1) as c:
                    load_x(c)
                load_x(CHUNKS - 1)
                general_sync()

            windows_fit(sp, windowed, general)

        @block.scalar
        def _(act):
            act.dma_start(w_dst[:, :], mw1[D:2 * D, :]).then_inc(s_wdst, 16)
            for n in range(4):
                part = slice(n * NODES // 4, (n + 1) * NODES // 4)
                act.dma_start(xc[0:D, part], x_t[:, part]).then_inc(s_xt, 16)
            act.dma_start(dst_i[:, :], dst_tiles).then_inc(s_dstt, 16)
            act.memzero(agg_t[:, :]).then_inc(s_zero_act, 1)
            act.memzero(xc[D:P, NODES // 2:]).then_inc(s_zero_act, 1)
            def open_update():
                act.wait_ge(s_wupd, 96)

            def windowed():
                act.wait_ge(s_xt, 64)
                for g, base in zip(range(2), window_bases(ET.Activation, 0, 2)):
                    pick_window(g, g, base)
                copy_x(0, 0)

                def lap(i, c):
                    first = i * UNROLL + 2
                    bases = window_bases(ET.Activation, first, min(UNROLL, G_END - first) if
                                         isinstance(i, int) else UNROLL)
                    for k in range(UNROLL):
                        g = i * UNROLL + k
                        if c is not None and k == 6:
                            act_square(c)
                        if exists(g + 1):
                            copy_x(g + 1, (k + 1) % UNROLL)
                        if exists(g + 2):
                            pick_window(g + 2, (k + 2) % UNROLL, bases[k])
                        if c is not None and k == 6:
                            act_deviation(c)
                        if exists(g):
                            relu(g, k)
                        if c is not None and k == 3:
                            act_relu(c)
                        if c is not None and k == 6:
                            act_store(c)
                laps(act, lap, open_update, act_chunks)

            def general():
                open_update()
                general_scalar()
                all_chunks(act, act_chunks)

            windows_fit(act, windowed, general)
            act.wait_ge(s_out, (CHUNKS + 1) * 16)

        @block.vector
        def _(dve):
            dve.memset(ones_bf[:, :], 1.0)
            dve.memset(src_idx[:, TILES:], 0)
            dve.memset(eps[:, :], EPS).then_inc(s_const, 1)
            dve.memset(xe[D + DE:KX, :, :], 1.0).then_inc(s_one_row, 1)
            dve.wait_ge(s_iota, 3)
            dve.tensor_copy(iota[:, :], iota_i[:, :])
            dve.tensor_copy(trash_f[:, :], trash_i[:, :])
            dve.tensor_copy(lag_f[:, :], lag_i[:, :]).then_inc(s_iotaf, 1)
            dve.wait_ge(s_ident, 2)
            dve.tensor_copy(ident_bf[:, :], ident[:, :]).then_inc(s_ident_bf, 1)
            dve.wait_ge(s_dstg, 16)
            dve.tensor_reduce(base_mn[:, :], dst_g.rearrange("p (g e) -> p g e", e=GE), X, ALU.min
                              ).then_inc(s_base, 1)
            dve.scalar_tensor_tensor(dst_g_real, dst_g, float(N_NODES), dst_g, ALU.is_lt, ALU.mult
                                     ).then_inc(s_base, 1)
            dve.wait_ge(s_base, 1)
            dve.tensor_scalar(base_f[:, :], base_mn[:, :], float(LAST_BASE), None, ALU.min
                              ).then_inc(s_win, 1)
            dve.wait_ge(s_base, 2)
            dve.reduce_max(dst_mx[:, :], dst_g_real.rearrange("p (g e) -> p g e", e=GE), X).then_inc(s_win, 1)
            dve.wait_ge(s_win, 2)
            dve.tensor_copy(base_i[:, :], base_f[:, :]).then_inc(s_win, 1)
            dve.tensor_tensor(spread[:, :], dst_mx[:, :], base_f[:, :], ALU.subtract).then_inc(s_win, 1)
            dve.wait_ge(s_iotaf, 1)
            dve.tensor_tensor(lag[:, :], lag_f[:, 0:1].to_broadcast([GROWS, GPP]), base_f[:, :],
                              ALU.subtract).then_inc(s_win, 1)
            dve.memset(xc[D:P, 0:NODES // 2], 0.0).then_inc(s_zero_dve, 1)
            dve.wait_ge(s_dstt, 16)
            dve.wait_ge(s_back, 64)
            grid = [P, GROUPS, TPG]
            dve.tensor_tensor(rel[:, :].rearrange("p (g j) -> p g j", j=TPG),
                              dst_i[:, :].rearrange("p (g j) -> p g j", j=TPG),
                              base_all[:, :, None].to_broadcast(grid), ALU.subtract).then_inc(s_rel, 1)
            dve.reduce_max(path[:, 0:1], spread_row[:, :], X).then_inc(s_flag, 1)
            dve.tensor_scalar(lag_row[:, :], lag_row[:, :], 0.0, None, ALU.max).then_inc(s_lag, 1)
            dve.wait_ge(s_lag, 1)
            dve.reduce_max(path[:, 1:2], lag_row[:, :], X).then_inc(s_flag, 1)
            dve.memset(resid[:, REAL_BLOCKS * D:], 0.0).then_inc(s_zero_w2, 1)
            dve.memset(w2_pad[:, 0:D], 0.0).then_inc(s_zero_w2, 1)

            def open_update():
                dve.wait_ge(s_wupd, 96)
                dve.wait_ge(s_resid, (CHUNKS + 1) * 16)

            def windowed():
                dve.wait_ge(s_rel, 1)
                dve.wait_ge(s_src, 16)
                one_hot(0, 0)
                one_hot(1, 1)
                copy_oh(0, 0)
                next_indices(0, 0)
                dve.wait_ge(s_zero_act, 2)
                dve.wait_ge(s_zero_dve, 1)

                def lap(i, c):
                    if isinstance(i, int) and i == 0:
                        bases = [None, None, *window_bases(ET.DVE, 0, UNROLL - 2)]
                    else:
                        bases = window_bases(ET.DVE, i * UNROLL - 2, UNROLL)
                    for k in range(UNROLL):
                        g = i * UNROLL + k
                        if exists(g + 2):
                            one_hot(g + 2, (k + 2) % UNROLL)
                        if exists(g + 1):
                            copy_oh(g + 1, (k + 1) % UNROLL)
                        if exists(g + 1 + UNROLL):
                            next_indices(g + 1, (k + 1) % UNROLL)
                        if not (isinstance(g, int) and g < 2):
                            add_window(g - 2, (k - 2) % UNROLL, bases[k])
                        if c is not None:
                            if k == 1:
                                dve_c2(c)
                            elif k == 2:
                                dve_stack(c)
                            elif k == 5:
                                dve_center(c)
                            elif k == 6:
                                dve_variance(c)
                                dve_normalize(c)
                    if isinstance(i, int) and i == ITERS - 1:
                        last = ITERS * UNROLL - 2
                        for g, base in zip(range(last, G_END), window_bases(ET.DVE, last, 2)):
                            add_window(g, g % UNROLL, base)
                laps(dve, lap, open_update, dve_chunks)

            def general():
                open_update()
                general_vector()
                all_chunks(dve, dve_chunks)

            windows_fit(dve, windowed, general)

        @block.tensor
        def _(pe):
            def open_update():
                pe.wait_ge(s_wupd, 96)

            def begin():
                pe.wait_ge(s_ident, 2)
                pe.wait_ge(s_wmsg, 48)
                pe.wait_ge(s_wdst, 16)
                pe.wait_ge(s_xt, 64)
                pe.wait_ge(s_one_row, 1)
                pe.wait_ge(s_const, 1)
                pe.wait_ge(s_ident_bf, 1)

            def windowed():
                begin()
                transpose_x(pe, 0, 0, 0)
                transpose_oh(pe, 0, 0)

                def lap(i, c):
                    for k in range(UNROLL):
                        g = i * UNROLL + k
                        if c is not None:
                            if k == 2:
                                pe_m1(c)
                            elif k == 3:
                                pe_m2(c)
                            elif k == 5:
                                pe_m3(c)
                        if exists(g + 1):
                            transpose_x(pe, g + 1, (k + 1) % UNROLL, i + (k + 1) // UNROLL)
                            transpose_oh(pe, g + 1, (k + 1) % UNROLL)
                        if exists(g):
                            hidden(pe, g, k, i)
                        if not (isinstance(g, int) and (g == 0 or g > G_END)):
                            aggregate(pe, g - 1, (k - 1) % UNROLL)
                laps(pe, lap, open_update, pe_chunks)

            def general():
                begin()
                open_update()
                general_tensor()
                all_chunks(pe, pe_chunks)

            windows_fit(pe, windowed, general)


def kernel(x, src, dst, edge_attr_32, L0_gnn_mW1, L0_gnn_mb1, L0_gnn_mW2, L0_gnn_mb2,
           L0_gnn_uW1, L0_gnn_ub1, L0_gnn_uW2, L0_gnn_ub2):
    import numpy as np
    import concourse.bacc as bacc
    from concourse.bass_utils import run_bass_kernel_spmd

    x, src, dst, edge = (np.asarray(a) for a in (x, src, dst, edge_attr_32))
    pad = EDGES - N_EDGES
    src_p = np.concatenate([src, np.zeros(pad, src.dtype)])
    dst_p = np.concatenate([dst, np.full(pad, N_NODES, dst.dtype)])
    edge_p = np.concatenate([edge, np.zeros((pad, DE), edge.dtype)])
    x_p = np.concatenate([x, np.zeros((NODES - N_NODES, D), x.dtype)])
    src_tiles = np.ascontiguousarray(src_p.reshape(TILES, P).T)
    arrays = {
        "x_rows": x,
        "x_t": np.ascontiguousarray(x_p.T),
        "src_first": np.ascontiguousarray(src_tiles[:, :UNROLL * TPG]),
        "src_all": src_tiles,
        "dst_groups": dst_p.reshape(GROWS, GPP * GE),
        "dst_tiles": np.ascontiguousarray(dst_p.reshape(TILES, P).T),
        "edge_t": np.ascontiguousarray(edge_p.T),
        "mw1": np.asarray(L0_gnn_mW1), "mb1": np.asarray(L0_gnn_mb1),
        "mw2": np.asarray(L0_gnn_mW2), "mb2": np.asarray(L0_gnn_mb2),
        "uw1": np.asarray(L0_gnn_uW1), "ub1": np.asarray(L0_gnn_ub1),
        "uw2": np.asarray(L0_gnn_uW2), "ub2": np.asarray(L0_gnn_ub2),
    }
    nc = bacc.Bacc("TRN2", target_bir_lowering=False, num_devices=1)
    args = [nc.dram_tensor(name, a.shape, mybir.dt.from_np(a.dtype), kind="ExternalInput").ap()
            for name, a in arrays.items()]
    out = nc.dram_tensor("out", (N_NODES, D), mybir.dt.float32, kind="ExternalOutput").ap()
    build(nc, *args, out)
    return run_bass_kernel_spmd(nc, [arrays], core_ids=[0]).results[0]["out"]
```
